# Optimizing a Trainium2 kernel written in Bass

```python
import numpy as np
import jax
import jax.numpy as jnp

def _softmax(x, axis=-1):
    return jax.nn.softmax(x, axis=axis)

def _gelu(x):
    return jax.nn.gelu(x, approximate=True)

def _silu(x):
    return jax.nn.silu(x)

def _sigmoid(x):
    return jax.nn.sigmoid(x)

def _layernorm(x, axis=-1, eps=1e-05):
    m = jnp.mean(x, axis=axis, keepdims=True)
    v = jnp.var(x, axis=axis, keepdims=True)
    return (x - m) / jnp.sqrt(v + eps)

def _scatter_add(tgt, idx, src, axis=0):
    return tgt.at[idx].add(src)

def _segment_sum(src, seg, n):
    return jax.ops.segment_sum(src, seg, n)
kernel_name = 'mk_xattn_ffn_d1_seqx_r4_7cbf67'

def setup_inputs(seed: int=0):
    np.random.seed(seed)
    _w = jnp.asarray

    def _rec_inputs():
        import jax
        import jax.numpy as jnp
        _rk = jax.random.key(seed)
        x = -0.0002928 + 1 * jax.random.normal(jax.random.fold_in(_rk, 1), (32, 256, 256), jnp.float32)
        _lenS = 256 - jax.random.randint(jax.random.fold_in(_rk, 7), (32,), 0, max(1, 256 // 4) + 1, jnp.int32)
        _lenS2 = 256 - jax.random.randint(jax.random.fold_in(_rk, 8), (32,), 0, max(1, 256 // 4) + 1, jnp.int32)
        _ctx_1024P = jax.random.normal(jax.random.fold_in(_rk, 11), (32, 16, 256), jnp.float32)
        _ctx_1024c = jax.random.dirichlet(jax.random.fold_in(_rk, 511), 0.3 * jnp.ones((16,), jnp.float32), (32, 256))
        _ctx_1024t = jnp.einsum('bsk,bkd->bsd', _ctx_1024c, _ctx_1024P)
        _ctx_1024t = _ctx_1024t * jax.lax.rsqrt(jnp.mean(jnp.square(_ctx_1024t)) + 1e-12) * 0.953939
        ctx_1024 = -1.39393e-06 + 0.999914 * (_ctx_1024t + 0.3 * jax.random.normal(jax.random.fold_in(_rk, 611), (32, 256, 256), jnp.float32))
        return (x, ctx_1024)
    x, ctx_1024 = _rec_inputs()

    def _L0_xattn_setup():
        import jax, jax.numpy as jnp
        import numpy as np
        B, N, QD, CD, H, DH = (2, 512, 256, 256, 8, 64)
        INNER = H * DH
        SCALE = DH ** (-0.5)

        def _split_heads(t):
            b, n, _ = t.shape
            return t.reshape(b, n, H, DH).transpose(0, 2, 1, 3)
        key = jax.random.key(seed)
        ks = jax.random.split(key, 11)
        s = lambda fan: 1.0 / np.sqrt(fan)
        return {'x': jax.random.normal(ks[0], (B, N, QD), jnp.float32), 'context': jax.random.normal(ks[1], (B, N, CD), jnp.float32), 'Wq1': jax.random.normal(ks[2], (QD, INNER), jnp.float32) * s(QD), 'Wk1': jax.random.normal(ks[3], (QD, INNER), jnp.float32) * s(QD), 'Wv1': jax.random.normal(ks[4], (QD, INNER), jnp.float32) * s(QD), 'Wq2': jax.random.normal(ks[5], (CD, INNER), jnp.float32) * s(CD), 'Wk2': jax.random.normal(ks[6], (CD, INNER), jnp.float32) * s(CD), 'Wv2': jax.random.normal(ks[7], (CD, INNER), jnp.float32) * s(CD), 'alpha_attn': jnp.zeros((), jnp.float32), 'Wout': jax.random.normal(ks[8], (INNER, QD), jnp.float32) * s(INNER), 'bout': jnp.zeros((QD,), jnp.float32)}
    _L0_xattn_all = _L0_xattn_setup()
    _L0_xattn_in = {k: v for k, v in _L0_xattn_all.items() if k in ('Wq1', 'Wk1', 'Wv1', 'Wq2', 'Wk2', 'Wv2', 'alpha_attn', 'Wout', 'bout')}
    del _L0_xattn_all

    def _L0_ffn_setup():
        import jax, jax.numpy as jnp
        import numpy as np
        N_EXPERTS = 16
        TOP_K = 4
        HIDDEN = 256
        INTER = 128
        B, S = (2, 256)
        key = jax.random.key(seed)
        k1, k2, k3, k4, k5 = jax.random.split(key, 5)
        return {'hidden_states': jax.random.normal(k1, (B, S, HIDDEN), dtype=jnp.float32), 'gate_w': jax.random.normal(k2, (N_EXPERTS, HIDDEN), dtype=jnp.float32) * 0.02, 'w1': jax.random.normal(k3, (N_EXPERTS, HIDDEN, INTER), dtype=jnp.float32) * 0.02, 'w3': jax.random.normal(k4, (N_EXPERTS, HIDDEN, INTER), dtype=jnp.float32) * 0.02, 'w2': jax.random.normal(k5, (N_EXPERTS, INTER, HIDDEN), dtype=jnp.float32) * 0.02}
    _L0_ffn_all = _L0_ffn_setup()
    _L0_ffn_in = {k: v for k, v in _L0_ffn_all.items() if k in ('gate_w', 'w1', 'w3', 'w2')}
    del _L0_ffn_all
    return {'x': x, 'ctx_1024': ctx_1024, 'L0_xattn_Wq1': _L0_xattn_in['Wq1'], 'L0_xattn_Wk1': _L0_xattn_in['Wk1'], 'L0_xattn_Wv1': _L0_xattn_in['Wv1'], 'L0_xattn_Wq2': _L0_xattn_in['Wq2'], 'L0_xattn_Wk2': _L0_xattn_in['Wk2'], 'L0_xattn_Wv2': _L0_xattn_in['Wv2'], 'L0_xattn_alpha_attn': _L0_xattn_in['alpha_attn'], 'L0_xattn_Wout': _L0_xattn_in['Wout'], 'L0_xattn_bout': _L0_xattn_in['bout'], 'L0_ffn_gate_w': _L0_ffn_in['gate_w'], 'L0_ffn_w1': _L0_ffn_in['w1'], 'L0_ffn_w3': _L0_ffn_in['w3'], 'L0_ffn_w2': _L0_ffn_in['w2']}

def reference(x, ctx_1024, L0_xattn_Wq1, L0_xattn_Wk1, L0_xattn_Wv1, L0_xattn_Wq2, L0_xattn_Wk2, L0_xattn_Wv2, L0_xattn_alpha_attn, L0_xattn_Wout, L0_xattn_bout, L0_ffn_gate_w, L0_ffn_w1, L0_ffn_w3, L0_ffn_w2):
    import jax
    import jax.numpy as jnp

    def _L0_xattn_ref(x, context, Wq1, Wk1, Wv1, Wq2, Wk2, Wv2, alpha_attn, Wout, bout):
        import jax, jax.numpy as jnp
        import numpy as np
        B, N, QD, CD, H, DH = (2, 512, 256, 256, 8, 64)
        INNER = H * DH
        SCALE = DH ** (-0.5)

        def _split_heads(t):
            b, n, _ = t.shape
            return t.reshape(b, n, H, DH).transpose(0, 2, 1, 3)
        q1 = _split_heads(x @ Wq1)
        k1 = _split_heads(x @ Wk1)
        v1 = _split_heads(x @ Wv1)
        q2 = _split_heads(context @ Wq2)
        k2 = _split_heads(context @ Wk2)
        v2 = _split_heads(context @ Wv2)
        sim1 = jnp.einsum('bhid,bhjd->bhij', q2, k1) * SCALE
        attn1 = jax.nn.softmax(sim1, axis=-1)
        out1 = jnp.einsum('bhij,bhjd->bhid', attn1, v1)
        sim2 = jnp.einsum('bhid,bhjd->bhij', q1, k2) * SCALE
        attn2 = jax.nn.softmax(sim2, axis=-1)
        out2 = jnp.einsum('bhij,bhjd->bhid', attn2, v2)
        alpha = jax.nn.sigmoid(alpha_attn)
        out = out1 * alpha + out2 * (1.0 - alpha)
        out = out.transpose(0, 2, 1, 3).reshape(out.shape[0], out.shape[2], INNER)
        return out @ Wout + bout

    def _L0_ffn_ref(hidden_states, gate_w, w1, w3, w2):
        import jax, jax.numpy as jnp
        import numpy as np
        N_EXPERTS = 16
        TOP_K = 4
        HIDDEN = 256
        INTER = 128
        B, S = (2, 256)
        'DeepseekV3 MoE adapter forward: router -> sparse scores -> expert GLU MLP -> combine.'
        b, s, h = hidden_states.shape
        x = hidden_states.reshape(-1, h)
        logits = jnp.einsum('th,eh->te', x, gate_w)
        probs = jax.nn.softmax(logits, axis=-1)
        topk_w, topk_idx = jax.lax.top_k(probs, TOP_K)
        topk_w = topk_w / jnp.sum(topk_w, axis=-1, keepdims=True)
        one_hot = (topk_idx[..., None] == jnp.arange(N_EXPERTS)).astype(topk_w.dtype)
        scores = jnp.einsum('tk,tke->te', topk_w, one_hot)
        g = jnp.einsum('th,ehi->tei', x, w1)
        u = jnp.einsum('th,ehi->tei', x, w3)
        act = jax.nn.silu(g) * u
        expert_out = jnp.einsum('tei,eih->teh', act, w2)
        out = jnp.einsum('teh,te->th', expert_out, scores)
        return out.reshape(b, s, h)
    x = x + _L0_xattn_ref(_layernorm(x, axis=-1), ctx_1024, L0_xattn_Wq1, L0_xattn_Wk1, L0_xattn_Wv1, L0_xattn_Wq2, L0_xattn_Wk2, L0_xattn_Wv2, L0_xattn_alpha_attn, L0_xattn_Wout, L0_xattn_bout)
    x = x + _L0_ffn_ref(_layernorm(x, axis=-1), L0_ffn_gate_w, L0_ffn_w1, L0_ffn_w3, L0_ffn_w2)
    return x

_drawn_inputs = setup_inputs


def setup_inputs(seed=0):
    import zlib

    import numpy as np

    out = dict(_drawn_inputs(seed))
    spreads = {'L0_xattn_bout': (0.0, 0.1)}
    factors = {'L0_ffn_gate_w': 8.0, 'L0_ffn_w1': 8.0, 'L0_ffn_w3': 8.0, 'L0_ffn_w2': 8.0}
    for name, (base, spread) in spreads.items():
        noise = np.random.default_rng([zlib.crc32(name.encode()), seed]).standard_normal(out[name].shape)
        drawn = base * np.exp(spread * noise) if base else spread * noise
        out[name] = jnp.asarray(drawn.astype(out[name].dtype))
    for name, factor in factors.items():
        out[name] = (out[name] * factor).astype(out[name].dtype)
    return out
```

```python
from contextlib import ExitStack

import concourse.bass as bass
from concourse import mybir

F32 = mybir.dt.float32
F32R = mybir.dt.float32r
U32 = mybir.dt.uint32
ALU = mybir.AluOpType
ACT = mybir.ActivationFunctionType
AX = mybir.AxisListType

P = 128
TOP_K = 4
EPS = 1e-5
HEAD_DIM = 64


def wait(eng, sem, count):
    if isinstance(count, int) and count <= 0:
        return
    eng.wait_ge(sem, count)


def xattn_moe_kernel(nc, x, ctx, Wq1, Wk1, Wv1, Wq2, Wk2, Wv2, alpha_attn, Wout, bout,
                     gate_w, w1, w3, w2, out):
    B, S, D = x.shape
    INNER = Wq1.shape[1]
    E, _, I = w1.shape
    KT = D // P
    ST = S // P
    PAIRS = INNER // P
    STEPS = 2 * PAIRS
    CHUNKS = ST * E // 2
    SCALE = HEAD_DIM ** -0.5
    assert S == 2 * P and D == 2 * P and INNER == 4 * P and I == P and E == 16 and STEPS * 2 == CHUNKS
    ROUTER_STEPS = 12

    with ExitStack() as stack:
        def sb(name, shape, dt=F32):
            return stack.enter_context(nc.sbuf_tensor(name, shape, dt))

        def ps(name, shape):
            return stack.enter_context(nc.psum_tensor(name, shape, F32))

        def sem(name):
            return stack.enter_context(nc.semaphore(name))

        PROJ = [Wq2, Wk2, Wv2, Wk1, Wq1, Wv1]
        wp = [sb("wp_hi", [P, 6, KT, INNER], F32R), sb("wp_lo", [P, 6, KT, INNER], F32R)]
        wgu = [sb("wgu_hi", [P, E, KT, 2, I], F32R), sb("wgu_lo", [P, E, KT, 2, I], F32R)]
        wdn = [sb("wdn_hi", [P, E, D], F32R), sb("wdn_lo", [P, E, D], F32R)]
        wgate = [sb("wgate_hi", [P, KT, E], F32R), sb("wgate_lo", [P, KT, E], F32R)]
        wout = sb("wout", [P, PAIRS, D])
        gate_rows = sb("gate_rows", [E, D])
        bias = sb("bias", [P, D])
        qT = [sb(f"qT{d}", [P, PAIRS, S]) for d in range(2)]
        kT = [sb(f"kT{d}", [P, PAIRS, S]) for d in range(2)]
        val = [sb(f"val{d}", [P, ST, INNER]) for d in range(2)]
        rows = sb("rows", [P, ST, D])
        rowsT = [sb("rowsT_hi", [P, KT, S], F32R), sb("rowsT_lo", [P, KT, S], F32R)]
        x_in = sb("x_in", [P, ST, D])
        x_res = sb("x_res", [P, ST, D])
        x_mid = sb("x_mid", [P, ST, D])
        probs = sb("probs", [P, 2, ST, S])
        probsT = sb("probsT", [P, 2, ST, S])
        attnT = sb("attnT", [P, PAIRS, S])
        moeT = [sb("moeT_hi", [P, KT, S], F32R), sb("moeT_lo", [P, KT, S], F32R)]
        gated = sb("gated", [P, 2, I])
        actT = [sb("actT_hi", [P, 2, P], F32R), sb("actT_lo", [P, 2, P], F32R)]
        ident = sb("ident", [P, P])
        alphas = sb("alphas", [P, 2])
        al = sb("al", [P, 2])
        mx = sb("mx", [P, 4])
        nmx = sb("nmx", [P, 4])
        sums = sb("sums", [P, 4])
        inv = sb("inv", [P, 4])
        rec = sb("rec", [P, 4])
        stats = sb("stats", [P, ST, 6])
        mv = sb("mv", [P, ST, 2])
        ve = sb("ve", [P, ST])
        rstd = sb("rstd", [P, ST])
        mhalf = sb("mhalf", [P, ST])
        lmax = sb("lmax", [P, ST])
        lexp = sb("lexp", [P, ST, E])
        pexp = sb("pexp", [P, ST, E])
        top = sb("top", [P, ST, 8])
        topi = sb("topi", [P, ST, 8], U32)
        topf = sb("topf", [P, ST, TOP_K])
        tsum = sb("tsum", [P, ST])
        trec = sb("trec", [P, ST])
        tw = sb("tw", [P, ST, TOP_K])
        onehot = sb("onehot", [P, ST, E, TOP_K])
        expert = sb("expert", [P, E])
        score = sb("score", [P, ST, E])

        p_rot = ps("p_rot", [P, 4, 2 * S])
        p_av = ps("p_av", [P, 2 * S])
        p_gu = ps("p_gu", [P, 2, 2, I])
        p_tr = ps("p_tr", [P, 2 * S])
        p_y = ps("p_y", [P, ST, D])

        piece_in = [sem(f"piece_in{i}") for i in range(4)]
        const_in, x_landed, ctx_landed, y_stored = (sem(n) for n in ("const_in", "x_landed", "ctx_landed", "y_stored"))
        consts_set, al_set, piece_hi, piece_lo, gate_t, gate_hi, gate_lo = (
            sem(n) for n in ("consts_set", "al_set", "piece_hi", "piece_lo", "gate_t", "gate_hi", "gate_lo"))
        ctx_t, x_t, rowsT_hi, rowsT_lo, proj_done, proj_out = (
            sem(n) for n in ("ctx_t", "x_t", "rowsT_hi_set", "rowsT_lo_set", "proj_done", "proj_out"))
        scores_done, nmx_set, mx_set, exp_done, inv_set, rec_set, normed, pt_done, pt_out_a, pt_out_b, av_done, attn_out = (
            sem(n) for n in ("scores_done", "nmx_set", "mx_set", "exp_done", "inv_set", "rec_set", "normed", "pt_done",
                             "pt_out_a", "pt_out_b", "av_done", "attn_out"))
        outp_done, mid_set = sem("outp_done"), sem("mid_set")
        stats_set, mv_set, ve_set, rstd_set, ln1_set, ln2_set, x_res_set = (
            sem(n) for n in ("stats_set", "mv_set", "ve_set", "rstd_set", "ln1_set", "ln2_set", "x_res_set"))
        moe_t, moeT_hi, moeT_lo, logits_done, logits_read, router_step, router_exp = (
            sem(n) for n in ("moe_t", "moeT_hi_set", "moeT_lo_set", "logits_done", "logits_read",
                             "router_step", "router_exp"))
        gu_done, tanh_done, gate_step, act_set, act_t, actT_hi, actT_lo, down_done, y_set = (
            sem(n) for n in ("gu_done", "tanh_done", "gate_step", "act_set", "act_t", "actT_hi_set",
                             "actT_lo_set", "down_done", "y_set"))

        p_gu_flat = p_gu[:, :, :, :].rearrange("p e g i -> p (e g i)")
        x_dram = x.rearrange("b (t p) d -> b p t d", p=P)
        ctx_dram = ctx.rearrange("b (t p) d -> b p t d", p=P)
        out_dram = out.rearrange("b (t p) d -> b p t d", p=P)

        slots = [qT[0], kT[0], qT[1], kT[1]]
        slot = [t[:, :, :].rearrange("p a b -> p (a b)") for t in slots]
        PIECE = PAIRS * S
        pieces = []
        for n, w in enumerate(PROJ):
            pieces.append(([(slot[len(pieces) % 4].rearrange("p (k n) -> p k n", k=KT),
                             w.rearrange("(k p) n -> p k n", p=P))],
                           [t[:, n, :, :].rearrange("p k n -> p (k n)") for t in wp]))
        for e in range(0, E, 2):
            v = slot[len(pieces) % 4].rearrange("p (e k g i) -> p e k g i", e=2, k=KT, g=2)
            pieces.append(([(v[:, j, :, g, :], w[e + j].rearrange("(k p) i -> p k i", p=P))
                            for j in range(2) for g, w in enumerate((w1, w3))],
                           [t[:, e:e + 2, :, :, :].rearrange("p e k g i -> p (e k g i)") for t in wgu]))
        for e in range(0, E, 4):
            pieces.append(([(slot[len(pieces) % 4].rearrange("p (e n) -> p e n", e=4),
                             w2[e:e + 4].rearrange("e p n -> p e n"))],
                           [t[:, e:e + 4, :].rearrange("p e n -> p (e n)") for t in wdn]))
        NP_ = len(pieces)

        def arrived(n):
            return 16 * sum(len(pieces[m][0]) for m in range(n % 4, n + 1, 4))

        N_CONST = 4

        block = stack.enter_context(nc.Block())

        def iterations(eng, body):
            body(0, True, False, False)
            body(1, True, True, False)
            with eng.Fori(2, B) as b:
                body(b, True, True, True)
            body(B, False, True, True)
            body(B + 1, False, False, True)

        def norm1(b):
            return 1 if isinstance(b, int) and b == 0 else 2 * b

        def norm2(b, cur):
            return 2 * b + 1 if cur else 2 * b

        @block.sync
        def _(sp):
            sp.dma_start(rows[:, :, :], ctx_dram[0]).then_inc(ctx_landed, 16)
            sp.dma_start(x_in[:, :, :], x_dram[0]).then_inc(x_landed, 16)
            sp.dma_start(gate_rows[:, :], gate_w).then_inc(const_in, 16)
            sp.dma_start(wout[:, :, :], Wout.rearrange("(c p) n -> p c n", p=P)).then_inc(const_in, 16)
            sp.dma_start(bias[:, :], bout.rearrange("(a n) -> a n", a=1).to_broadcast([P, D])).then_inc(const_in, 16)
            sp.dma_start(al[:, 0:1], alpha_attn.rearrange("(a n) -> a n", a=1).to_broadcast([P, 1])).then_inc(const_in, 16)
            for n, (loads, _) in enumerate(pieces):
                if n >= 4:
                    sp.wait_ge(piece_lo, n - 3)
                for dst, src in loads:
                    sp.dma_start(dst, src).then_inc(piece_in[n % 4], 16)

            def iteration(b, load, store):
                if load:
                    if isinstance(b, int) and b == 0:
                        sp.wait_ge(x_t, 1)
                    else:
                        sp.wait_ge(moe_t, b)
                    sp.dma_start(rows[:, :, :], ctx_dram[b + 1]).then_inc(ctx_landed, 16)
                if store:
                    sp.wait_ge(y_set, b - 1)
                    sp.dma_start(out_dram[b - 2], x_mid[:, :, :]).then_inc(y_stored, 16)
                if load:
                    sp.wait_ge(ln1_set, b + 1)
                    sp.wait_ge(x_res_set, b + 1)
                    sp.dma_start(x_in[:, :, :], x_dram[b + 1]).then_inc(x_landed, 16)

            iteration(0, True, False)
            iteration(1, True, False)
            with sp.Fori(2, B - 1) as b:
                sp.wait_ge(y_set, b - 1)
                sp.dma_start(out_dram[b - 2], x_mid[:, :, :]).then_inc(y_stored, 16)
                iteration(b, True, False)
            for b in range(B - 1, B + 2):
                iteration(b, False, True)
            sp.wait_ge(y_stored, 16 * B)

        @block.gpsimd
        def _(pool):
            pool.memset(ident[:, :], 0.0).then_inc(consts_set, 1)
            pool.wait_ge(consts_set, 1)
            pool.affine_select(out=ident[:, :], in_=ident[:, :], compare_op=ALU.not_equal, fill=1.0,
                               base=0, pattern=[[-1, P]], channel_multiplier=1).then_inc(consts_set, 1)
            pool.memset(mhalf[:, :], -0.5).then_inc(consts_set, 1)
            pool.iota(expert[:, :], [[1, E]], base=0, channel_multiplier=0,
                      allow_small_or_imprecise_dtypes=True).then_inc(consts_set, 1)
            pool.wait_ge(const_in, 16 * N_CONST)

            def rsqrt(n):
                pool.wait_ge(ve_set, n)
                pool.tensor_tensor(rstd[:, :], ve[:, :], mhalf[:, :], ALU.pow).then_inc(rstd_set, 1)

            def iteration(b, cur, prev, last):
                if cur:
                    rsqrt(norm1(b))
                if prev:
                    rsqrt(norm2(b, cur))
                if cur:
                    wait(pool, mid_set, b)
                    pool.wait_ge(x_landed, 16 * (b + 1))
                    pool.tensor_tensor(x_res[:, :, :], x_in[:, :, :],
                                       bias[:, :].unsqueeze(1).to_broadcast([P, ST, D]),
                                       ALU.add).then_inc(x_res_set, 1)
                    for u in range(STEPS):
                        pool.wait_ge(rec_set, STEPS * b + u + 1)
                        pool.tensor_tensor(probs[:, 0, 0, :], probs[:, 0, 0, :], rec[:, 0:1].to_broadcast([P, S]),
                                           ALU.mult).then_inc(normed, 1)
                        for g in range(1, 4):
                            h, t = g // 2, g % 2
                            pool.tensor_scalar(probs[:, h, t, :], probs[:, h, t, :], rec[:, g:g + 1], None,
                                               ALU.mult).then_inc(normed, 1)

            iterations(pool, iteration)

        @block.scalar
        def _(act):
            act.wait_ge(const_in, 16 * N_CONST)
            act.activation(al[:, 1:2], al[:, 0:1], ACT.Tanh, scale=0.5).then_inc(al_set, 1)
            for n, (_, parts) in enumerate(pieces):
                act.wait_ge(piece_in[n % 4], arrived(n))
                act.copy(parts[0], slot[n % 4]).then_inc(piece_hi, 1)
            act.wait_ge(gate_t, 1)
            act.copy(wgate[0][:, :, :].rearrange("p k e -> p (k e)"), p_gu_flat[:, 0:KT * E]).then_inc(gate_hi, 1)

            def proj_evac(b, n, dst, bank):
                act.wait_ge(proj_done, 12 * b + n + 1)
                if n == 0 and isinstance(b, int) and b == 0:
                    act.wait_ge(piece_lo, NP_)
                act.copy(dst, p_rot[:, bank, :]).then_inc(proj_out, 1)

            def moe_hi(m, s):
                act.wait_ge(act_t, CHUNKS * m + s + 1)
                wait(act, down_done, CHUNKS * m + s)
                act.copy(actT[0][:, :, :].rearrange("p e t -> p (e t)"), p_tr[:, 0:S]).then_inc(actT_hi, 1)

            def moe_tanh(m, s):
                act.wait_ge(gu_done, CHUNKS * m + s + 1)
                wait(act, act_t, CHUNKS * m + s)
                act.activation(gated[:, :, :], p_gu[:, :, 0, :], ACT.Tanh, scale=0.5).then_inc(tanh_done, 1)

            def probsT_out(b, u):
                act.wait_ge(pt_done, 2 * (STEPS * b + u) + 1)
                wait(act, av_done, STEPS * b + u)
                act.copy(probsT[:, 0, :, :].rearrange("p a b -> p (a b)"), p_rot[:, 2, :]).then_inc(pt_out_a, 1)

            def attn_evac(b, p):
                act.wait_ge(av_done, STEPS * b + 2 * p + 2)
                act.copy(attnT[:, p, :], p_av[:, 0:S]).then_inc(attn_out, 1)

            def flat(ap):
                return ap.rearrange("p a b -> p (a b)")

            def iteration(b, cur, prev, last):
                pb, lb = b - 1, b - 2
                if last:
                    moe_hi(lb, CHUNKS - 1)
                if prev:
                    probsT_out(pb, STEPS - 1)
                if cur:
                    act.wait_ge(ctx_t, b + 1)
                    wait(act, proj_done, 12 * b)
                    act.copy(flat(rowsT[0][:, :, :]), p_rot[:, 0, :]).then_inc(rowsT_hi, 1)
                    proj_evac(b, 0, flat(qT[0][:, 0:2, :]), 1)
                if prev:
                    attn_evac(pb, PAIRS - 1)
                if cur:
                    proj_evac(b, 1, flat(qT[0][:, 2:4, :]), 2)
                    proj_evac(b, 2, flat(kT[1][:, 0:2, :]), 3)
                    proj_evac(b, 3, flat(kT[1][:, 2:4, :]), 0)
                    proj_evac(b, 4, val[1][:, 0, :], 1)
                    proj_evac(b, 5, val[1][:, 1, :], 2)
                    act.wait_ge(x_t, b + 1)
                    act.copy(flat(rowsT[0][:, :, :]), p_rot[:, 3, :]).then_inc(rowsT_hi, 1)
                    proj_evac(b, 6, flat(kT[0][:, 0:2, :]), 0)
                    proj_evac(b, 7, flat(kT[0][:, 2:4, :]), 1)
                    proj_evac(b, 8, flat(qT[1][:, 0:2, :]), 2)
                if prev:
                    act.wait_ge(moe_t, pb + 1)
                    wait(act, gu_done, CHUNKS * pb)
                    act.copy(flat(moeT[0][:, :, :]), p_tr[:, :]).then_inc(moeT_hi, 1)
                if cur:
                    proj_evac(b, 9, flat(qT[1][:, 2:4, :]), 3)
                    proj_evac(b, 10, val[0][:, 0, :], 0)
                if prev:
                    act.wait_ge(logits_read, pb + 1)
                    wait(act, router_step, ROUTER_STEPS * pb)
                    act.activation(pexp[:, :, :], lexp[:, :, :], ACT.Exp).then_inc(router_exp, 1)
                if cur:
                    proj_evac(b, 11, val[0][:, 1, :], 1)
                for u in range(STEPS):
                    if prev and u:
                        moe_hi(pb, 2 * u - 1)
                    if cur and u:
                        probsT_out(b, u - 1)
                    if cur:
                        act.wait_ge(nmx_set, STEPS * b + u + 1)
                        wait(act, pt_done, 2 * (STEPS * b + u))
                        wait(act, inv_set, STEPS * b + u)
                    for g in range(4):
                        h, t = g // 2, g % 2
                        if prev and g == 2:
                            moe_tanh(pb, 2 * u)
                        if cur:
                            act.activation(probs[:, h, t, :], p_rot[:, h, t * S:(t + 1) * S], ACT.Exp,
                                           bias=nmx[:, g:g + 1], scale=SCALE,
                                           accum_out=sums[:, g:g + 1]).then_inc(exp_done, 1)
                    if cur and u and u % 2 == 0:
                        attn_evac(b, u // 2 - 1)
                    if prev:
                        moe_hi(pb, 2 * u)
                        moe_tanh(pb, 2 * u + 1)

            iterations(act, iteration)

        @block.vector
        def _(dve):
            dve.wait_ge(al_set, 1)
            dve.tensor_scalar(alphas[:, 0:1], al[:, 1:2], 0.5, 0.5, ALU.mult, ALU.add).then_inc(al_set, 1)
            dve.tensor_scalar(alphas[:, 1:2], al[:, 1:2], -0.5, 0.5, ALU.mult, ALU.add).then_inc(al_set, 1)
            for n, (_, parts) in enumerate(pieces):
                dve.wait_ge(piece_hi, n + 1)
                dve.tensor_tensor(parts[1], slot[n % 4], parts[0].bitcast(F32), ALU.subtract).then_inc(piece_lo, 1)
            dve.wait_ge(gate_hi, 1)
            dve.tensor_tensor(wgate[1][:, :, :].rearrange("p k e -> p (k e)"), p_gu_flat[:, 0:KT * E],
                              wgate[0][:, :, :].rearrange("p k e -> p (k e)").bitcast(F32),
                              ALU.subtract).then_inc(gate_lo, 1)

            def flat(ap):
                return ap.rearrange("p a b -> p (a b)")

            def moe_lo(m, s):
                dve.wait_ge(actT_hi, CHUNKS * m + s + 1)
                wait(dve, down_done, CHUNKS * m + s)
                dve.tensor_tensor(flat(actT[1][:, :, :]), p_tr[:, 0:S], flat(actT[0][:, :, :]).bitcast(F32),
                                  ALU.subtract).then_inc(actT_lo, 1)

            def moe_gate(m, s):
                t, e = s % ST, 2 * (s // ST)
                dve.wait_ge(tanh_done, CHUNKS * m + s + 1)
                dve.scalar_tensor_tensor(gated[:, :, :], gated[:, :, :], 1.0, p_gu[:, :, 0, :],
                                         ALU.add, ALU.mult).then_inc(gate_step, 1)
                if s == 0:
                    dve.wait_ge(router_step, ROUTER_STEPS * (m + 1))
                dve.wait_ge(gate_step, CHUNKS * m + s + 1)
                for j in range(2):
                    last = dve.scalar_tensor_tensor(gated[:, j, :], gated[:, j, :], score[:, t, e + j:e + j + 1],
                                                    p_gu[:, j, 1, :], ALU.mult, ALU.mult)
                last.then_inc(act_set, 1)

            def probsT_out(b, u):
                dve.wait_ge(pt_done, 2 * (STEPS * b + u) + 2)
                wait(dve, av_done, STEPS * b + u)
                dve.tensor_copy(flat(probsT[:, 1, :, :]), p_rot[:, 3, :]).then_inc(pt_out_b, 1)

            def layer_norm(n, src, free, count, done):
                for t in range(ST):
                    last = dve.bn_stats(stats[:, t, :], src[:, t, :])
                last.then_inc(stats_set, 1)
                dve.wait_ge(consts_set, 4)
                dve.wait_ge(stats_set, n)
                for t in range(ST):
                    last = dve.bn_aggr(mv[:, t, :], stats[:, t, :])
                last.then_inc(mv_set, 1)
                dve.wait_ge(mv_set, n)
                dve.tensor_scalar(ve[:, :], mv[:, :, 1], EPS, None, ALU.add).then_inc(ve_set, 1)
                dve.wait_ge(rstd_set, n)
                wait(dve, free, count)
                for t in range(ST):
                    last = dve.tensor_scalar(rows[:, t, :], src[:, t, :], mv[:, t, 0:1], rstd[:, t:t + 1],
                                             ALU.subtract, ALU.mult)
                last.then_inc(done, 1)

            def router(m):
                step = ROUTER_STEPS * m

                def bc(ap, axis, shape):
                    return ap.unsqueeze(axis).to_broadcast(shape)

                dve.wait_ge(logits_done, m + 1)
                logits = p_gu_flat[:, 0:ST * E].rearrange("p (t e) -> p t e", t=ST)
                dve.tensor_reduce(lmax[:, :], logits, AX.X, ALU.max).then_inc(router_step, 1)
                dve.wait_ge(router_step, step + 1)
                dve.tensor_tensor(lexp[:, :, :], logits, bc(lmax[:, :], 2, [P, ST, E]),
                                  ALU.subtract).then_inc(logits_read, 1)
                dve.wait_ge(consts_set, 4)
                dve.wait_ge(router_exp, m + 1)
                for t in range(ST):
                    dve.max(top[:, t, :], pexp[:, t, :]).then_inc(router_step, 1)
                dve.wait_ge(router_step, step + 3)
                dve.tensor_reduce(tsum[:, :], top[:, :, 0:TOP_K], AX.X, ALU.add).then_inc(router_step, 1)
                for t in range(ST):
                    dve.max_index(topi[:, t, :], top[:, t, :], pexp[:, t, :]).then_inc(router_step, 1)
                dve.wait_ge(router_step, step + 6)
                dve.tensor_copy(topf[:, :, :], topi[:, :, 0:TOP_K]).then_inc(router_step, 1)
                dve.reciprocal(trec[:, :], tsum[:, :]).then_inc(router_step, 1)
                dve.wait_ge(router_step, step + 8)
                dve.tensor_tensor(onehot[:, :, :, :], bc(bc(expert[:, :], 1, [P, ST, E]), 3, [P, ST, E, TOP_K]),
                                  bc(topf[:, :, :], 2, [P, ST, E, TOP_K]), ALU.is_equal).then_inc(router_step, 1)
                dve.scalar_tensor_tensor(tw[:, :, :], top[:, :, 0:TOP_K], 0.5, bc(trec[:, :], 2, [P, ST, TOP_K]),
                                         ALU.mult, ALU.mult).then_inc(router_step, 1)
                dve.wait_ge(router_step, step + 10)
                dve.tensor_tensor(onehot[:, :, :, :], onehot[:, :, :, :], bc(tw[:, :, :], 2, [P, ST, E, TOP_K]),
                                  ALU.mult).then_inc(router_step, 1)
                dve.wait_ge(router_step, step + 11)
                dve.tensor_reduce(score[:, :, :], onehot[:, :, :, :], AX.X, ALU.add).then_inc(router_step, 1)

            def iteration(b, cur, prev, last):
                pb, lb = b - 1, b - 2
                if last:
                    moe_lo(lb, CHUNKS - 1)
                if prev:
                    probsT_out(pb, STEPS - 1)
                if last:
                    dve.wait_ge(down_done, CHUNKS * (lb + 1))
                    dve.tensor_tensor(flat(x_mid[:, :, :]), flat(p_y[:, :, :]), flat(x_mid[:, :, :]),
                                      ALU.add).then_inc(y_set, 1)
                if cur:
                    dve.wait_ge(rowsT_hi, 2 * b + 1)
                    wait(dve, proj_done, 12 * b)
                    dve.tensor_tensor(flat(rowsT[1][:, :, :]), p_rot[:, 0, :],
                                      flat(rowsT[0][:, :, :]).bitcast(F32), ALU.subtract).then_inc(rowsT_lo, 1)
                    dve.wait_ge(x_landed, 16 * (b + 1))
                    layer_norm(norm1(b), x_in, ctx_t, b + 1, ln1_set)
                    dve.wait_ge(rowsT_hi, 2 * b + 2)
                    dve.wait_ge(proj_done, 12 * b + 6)
                    dve.tensor_tensor(flat(rowsT[1][:, :, :]), p_rot[:, 3, :],
                                      flat(rowsT[0][:, :, :]).bitcast(F32), ALU.subtract).then_inc(rowsT_lo, 1)
                if prev:
                    dve.wait_ge(outp_done, pb + 1)
                    dve.wait_ge(x_res_set, pb + 1)
                    if last:
                        dve.wait_ge(y_stored, 16 * (lb + 1))
                    dve.tensor_tensor(flat(x_mid[:, :, :]), p_av[:, :], flat(x_res[:, :, :]),
                                      ALU.add).then_inc(mid_set, 1)
                    dve.wait_ge(mid_set, pb + 1)
                    layer_norm(norm2(b, cur), x_mid, x_t, b + 1 if cur else b, ln2_set)
                    dve.wait_ge(moeT_hi, pb + 1)
                    wait(dve, gu_done, CHUNKS * pb)
                    dve.tensor_tensor(flat(moeT[1][:, :, :]), p_tr[:, :],
                                      flat(moeT[0][:, :, :]).bitcast(F32), ALU.subtract).then_inc(moeT_lo, 1)
                    router(pb)
                for u in range(STEPS):
                    if cur:
                        dve.wait_ge(scores_done, STEPS * b + u + 1)
                        dve.tensor_reduce(mx[:, :], p_rot[:, 0:2, :].rearrange("p h (t k) -> p (h t) k", t=ST),
                                          AX.X, ALU.max).then_inc(mx_set, 1)
                        dve.wait_ge(mx_set, STEPS * b + u + 1)
                        wait(dve, exp_done, 4 * (STEPS * b + u))
                        dve.tensor_scalar(nmx[:, :], mx[:, :], -SCALE, None, ALU.mult).then_inc(nmx_set, 1)
                    if prev and u:
                        moe_lo(pb, 2 * u - 1)
                    if cur and u:
                        probsT_out(b, u - 1)
                    if prev:
                        moe_gate(pb, 2 * u)
                    if cur:
                        dve.wait_ge(exp_done, 4 * (STEPS * b + u + 1))
                        dve.reciprocal(inv[:, :], sums[:, :]).then_inc(inv_set, 1)
                        dve.wait_ge(inv_set, STEPS * b + u + 1)
                        wait(dve, normed, 4 * (STEPS * b + u))
                        dve.tensor_scalar(rec[:, :], inv[:, :], alphas[:, u % 2:u % 2 + 1], None,
                                          ALU.mult).then_inc(rec_set, 1)
                    if prev:
                        moe_lo(pb, 2 * u)
                        moe_gate(pb, 2 * u + 1)

            iterations(dve, iteration)

        @block.tensor
        def _(pe):
            pe.wait_ge(consts_set, 4)
            pe.wait_ge(const_in, 16 * N_CONST)
            for k in range(KT):
                last = pe.transpose(p_gu_flat[:, k * E:(k + 1) * E], gate_rows[:, k * P:(k + 1) * P], ident[0:E, 0:E])
            last.then_inc(gate_t, 1)

            PASSES = ((0, 0), (0, 1), (1, 0))

            def transpose_rows(dst):
                for k in range(KT):
                    for t in range(ST):
                        mm = pe.transpose(dst[:, k * S + t * P:k * S + (t + 1) * P],
                                          rows[:, t, k * P:(k + 1) * P], ident[:, :])
                return mm

            def project_cols(w, pair0, bank):
                for j in range(2):
                    c = (pair0 + j) * P
                    n = 0
                    for k in range(KT):
                        for a, r in PASSES:
                            mm = pe.matmul(p_rot[:, bank, j * S:(j + 1) * S], wp[a][:, w, k, c:c + P], rowsT[r][:, k, :],
                                           start=(n == 0), stop=(n == 5))
                            n += 1
                mm.then_inc(proj_done, 1)

            def project_rows(w, t, bank):
                n = 0
                for k in range(KT):
                    for r, a in PASSES:
                        mm = pe.matmul(p_rot[:, bank, :], rowsT[r][:, k, t * P:(t + 1) * P], wp[a][:, w, k, :],
                                       start=(n == 0), stop=(n == 5))
                        n += 1
                mm.then_inc(proj_done, 1)

            def scores(b, u):
                p, d = u // 2, u % 2
                if u == 0:
                    pe.wait_ge(proj_out, 12 * (b + 1))
                else:
                    pe.wait_ge(exp_done, 4 * (STEPS * b + u))
                for t in range(ST):
                    for h in range(2):
                        r = HEAD_DIM * h
                        mm = pe.matmul(p_rot[:, h, t * S:(t + 1) * S],
                                       qT[d][r:r + HEAD_DIM, p, t * P:(t + 1) * P],
                                       kT[d][r:r + HEAD_DIM, p, :], start=True, stop=True)
                mm.then_inc(scores_done, 1)

            def probs_t(b, u):
                pe.wait_ge(normed, 4 * (STEPS * b + u + 1))
                if u == 0:
                    pe.wait_ge(proj_out, 12 * b + 10)
                else:
                    pe.wait_ge(pt_out_a, STEPS * b + u)
                    pe.wait_ge(pt_out_b, STEPS * b + u)
                for h in range(2):
                    for k in range(ST):
                        for t in range(ST):
                            mm = pe.transpose(p_rot[:, 2 + h, k * S + t * P:k * S + (t + 1) * P],
                                              probs[:, h, t, k * P:(k + 1) * P], ident[:, :])
                    mm.then_inc(pt_done, 1)

            def attend(b, u):
                p, d = u // 2, u % 2
                pe.wait_ge(pt_out_a, STEPS * b + u + 1)
                pe.wait_ge(pt_out_b, STEPS * b + u + 1)
                if d == 0 and p:
                    pe.wait_ge(attn_out, PAIRS * b + p)
                if u == 0:
                    wait(pe, mid_set, b)
                for k in range(ST):
                    for h in range(2):
                        r = HEAD_DIM * h
                        c = p * P + r
                        mm = pe.matmul(p_av[r:r + HEAD_DIM, 0:S], val[d][:, k, c:c + HEAD_DIM], probsT[:, h, k, :],
                                       start=(d == 0 and k == 0), stop=(d == 1 and k == ST - 1),
                                       skip_group_check=True)
                mm.then_inc(av_done, 1)

            def out_project(b):
                pe.wait_ge(attn_out, PAIRS * (b + 1))
                for t in range(ST):
                    for c in range(PAIRS):
                        mm = pe.matmul(p_av[:, t * D:(t + 1) * D], attnT[:, c, t * P:(t + 1) * P], wout[:, c, :],
                                       start=(c == 0), stop=(c == PAIRS - 1))
                mm.then_inc(outp_done, 1)

            def logits(m):
                pe.wait_ge(moeT_lo, m + 1)
                wait(pe, act_set, CHUNKS * m)
                for t in range(ST):
                    n = 0
                    for k in range(KT):
                        for r, a in PASSES:
                            mm = pe.matmul(p_gu_flat[:, t * E:(t + 1) * E], moeT[r][:, k, t * P:(t + 1) * P],
                                           wgate[a][:, k, :], start=(n == 0), stop=(n == 5))
                            n += 1
                mm.then_inc(logits_done, 1)

            def gate_up(m, s):
                t, e = s % ST, 2 * (s // ST)
                if s == 0:
                    pe.wait_ge(logits_read, m + 1)
                else:
                    pe.wait_ge(act_set, CHUNKS * m + s)
                n = 0
                for k in range(KT):
                    for r, a in PASSES:
                        mm = pe.matmul(p_gu[:, :, :, :].rearrange("p e g i -> p e (g i)"),
                                       moeT[r][:, k, t * P:(t + 1) * P],
                                       wgu[a][:, e:e + 2, k, :, :].rearrange("p e g i -> p e (g i)"),
                                       start=(n == 0), stop=(n == 5))
                        n += 1
                mm.then_inc(gu_done, 1)

            def act_transpose(m, s):
                pe.wait_ge(act_set, CHUNKS * m + s + 1)
                if s == 0:
                    pe.wait_ge(moeT_lo, m + 1)
                else:
                    pe.wait_ge(actT_lo, CHUNKS * m + s)
                for j in range(2):
                    mm = pe.transpose(p_tr[:, j * P:(j + 1) * P], gated[:, j, :], ident[:, :])
                mm.then_inc(act_t, 1)

            def down(m, s):
                t, e = s % ST, 2 * (s // ST)
                pe.wait_ge(actT_lo, CHUNKS * m + s + 1)
                if s == 0:
                    wait(pe, y_set, m)
                for j in range(2):
                    for n, (r, a) in enumerate(PASSES):
                        mm = pe.matmul(p_y[:, t, :], actT[r][:, j, :], wdn[a][:, e + j, :],
                                       start=(s == 0 and j == 0 and n == 0),
                                       stop=(s >= CHUNKS - ST and j == 1 and n == 2), skip_group_check=True)
                mm.then_inc(down_done, 1)

            def iteration(b, cur, prev, last):
                pb, lb = b - 1, b - 2
                if last:
                    act_transpose(lb, CHUNKS - 1)
                if cur:
                    pe.wait_ge(ctx_landed, 16 * (b + 1))
                    wait(pe, exp_done, 4 * STEPS * b)
                    transpose_rows(p_rot[:, 0, :]).then_inc(ctx_t, 1)
                if prev:
                    probs_t(pb, STEPS - 1)
                if last:
                    down(lb, CHUNKS - 1)
                if cur:
                    pe.wait_ge(rowsT_lo, 2 * b + 1)
                    if isinstance(b, int) and b == 0:
                        pe.wait_ge(piece_lo, NP_)
                    project_cols(0, 0, 1)
                if prev:
                    attend(pb, STEPS - 1)
                if cur:
                    wait(pe, pt_out_a, STEPS * b)
                    project_cols(0, 2, 2)
                    wait(pe, pt_out_b, STEPS * b)
                    project_cols(1, 0, 3)
                    project_cols(1, 2, 0)
                    pe.wait_ge(proj_out, 12 * b + 1)
                    project_rows(2, 0, 1)
                    pe.wait_ge(proj_out, 12 * b + 2)
                    project_rows(2, 1, 2)
                    pe.wait_ge(ln1_set, b + 1)
                    pe.wait_ge(proj_out, 12 * b + 3)
                    transpose_rows(p_rot[:, 3, :]).then_inc(x_t, 1)
                if prev:
                    out_project(pb)
                if cur:
                    pe.wait_ge(rowsT_lo, 2 * b + 2)
                    for n in range(3):
                        pe.wait_ge(proj_out, 12 * b + 4 + n)
                        project_cols(3 + n // 2, 2 * (n % 2), n)
                if prev:
                    pe.wait_ge(ln2_set, pb + 1)
                    wait(pe, actT_lo, CHUNKS * pb)
                    transpose_rows(p_tr[:, :]).then_inc(moe_t, 1)
                if cur:
                    project_cols(4, 2, 3)
                    pe.wait_ge(proj_out, 12 * b + 7)
                    project_rows(5, 0, 0)
                if prev:
                    logits(pb)
                if cur:
                    pe.wait_ge(proj_out, 12 * b + 8)
                    project_rows(5, 1, 1)
                for u in range(STEPS):
                    if cur:
                        scores(b, u)
                    if prev and u:
                        act_transpose(pb, 2 * u - 1)
                    if cur and u:
                        probs_t(b, u - 1)
                    if prev:
                        gate_up(pb, 2 * u)
                        if u:
                            down(pb, 2 * u - 1)
                    if cur and u:
                        attend(b, u - 1)
                    if prev:
                        act_transpose(pb, 2 * u)
                        gate_up(pb, 2 * u + 1)
                        down(pb, 2 * u)

            iterations(pe, iteration)


_INS = ['x', 'ctx_1024', 'L0_xattn_Wq1', 'L0_xattn_Wk1', 'L0_xattn_Wv1', 'L0_xattn_Wq2', 'L0_xattn_Wk2',
        'L0_xattn_Wv2', 'L0_xattn_alpha_attn', 'L0_xattn_Wout', 'L0_xattn_bout', 'L0_ffn_gate_w', 'L0_ffn_w1',
        'L0_ffn_w3', 'L0_ffn_w2']


def kernel(**inputs):
    import numpy as _np
    import concourse.bacc as _bacc
    from concourse import mybir as _mybir
    from concourse.bass_utils import run_bass_kernel_spmd as _run

    nc = _bacc.Bacc("TRN2", target_bir_lowering=False, num_devices=1)
    arrays, args = {}, []
    for name in _INS:
        a = _np.ascontiguousarray(inputs[name])
        arrays[f"in_{name}_dram"] = a
        args.append(nc.dram_tensor(f"in_{name}_dram", a.shape, _mybir.dt.from_np(a.dtype), kind="ExternalInput").ap())
    shape = _np.shape(inputs["x"])
    args.append(nc.dram_tensor("out_0_dram", shape, _mybir.dt.float32, kind="ExternalOutput").ap())
    xattn_moe_kernel(nc, *args)
    r = _run(nc, [arrays], core_ids=[0])
    return r.results[0]["out_0_dram"]
```

```python
from contextlib import ExitStack

import concourse.bass as bass
from concourse import mybir

F32 = mybir.dt.float32
F32R = mybir.dt.float32r
U32 = mybir.dt.uint32
I32 = mybir.dt.int32
BF16 = mybir.dt.bfloat16
ALU = mybir.AluOpType
ACT = mybir.ActivationFunctionType
AX = mybir.AxisListType

P = 128
TOP_K = 4
EPS = 1e-5
HEAD_DIM = 64


def wait_alone(eng, sem, count):
    eng.wait_ge(sem, count)
    eng.nop(nofuse=True)


def flat(ap):
    names = " ".join("abcd"[:len(ap.shape) - 1])
    return ap.rearrange(f"p {names} -> p ({names})")


def spread(ap, axis, shape):
    return ap.unsqueeze(axis).to_broadcast(shape)


def wait(eng, sem, count):
    if isinstance(count, int) and count <= 0:
        return
    eng.wait_ge(sem, count)


def xattn_moe_kernel(nc, x, ctx, Wq1, Wk1, Wv1, Wq2, Wk2, Wv2, alpha_attn, Wout, bout,
                     gate_w, w1, w3, w2, out):
    B, S, D = x.shape
    INNER = Wq1.shape[1]
    E, _, I = w1.shape
    KT = D // P
    ST = S // P
    PAIRS = INNER // P
    STEPS = 2 * PAIRS
    PROJS = 6 * INNER * KT // 512
    SCALE = HEAD_DIM ** -0.5
    TOKENS = B * S
    TT = TOKENS // P
    GROUP = 2 * P
    REGION = TOKENS + GROUP
    ROW = D + 4
    GROUPS = TOKENS * TOP_K // GROUP + E
    MOST = TOKENS // GROUP
    DUMP = TOKENS * TOP_K
    LOADS = 8
    TC = -(-GROUPS // P)
    assert S == 2 * P and D == 2 * P and INNER == 4 * P and I == P and B >= 4 and B % 4 == 0
    assert GROUPS % LOADS == 0 and GROUPS >= 3 * LOADS
    ROUTER_STEPS = 19

    x_rows = nc.dram_tensor("x_rows", [E * REGION + E * GROUP, ROW], F32, kind="Internal").ap()
    y_rows = nc.dram_tensor("y_rows", [DUMP + 2 * E * GROUP, D], F32, kind="Internal").ap()
    mid_rows = nc.dram_tensor("mid_rows", [TOKENS, D], F32, kind="Internal").ap()
    tile_table = nc.dram_tensor("tile_table", [2, TC * P], I32, kind="Internal").ap()

    with ExitStack() as stack:
        def sb(name, shape, dt=F32, stack=stack):
            return stack.enter_context(nc.sbuf_tensor(name, shape, dt))

        def ps(name, shape, dt=F32, stack=stack):
            return stack.enter_context(nc.psum_tensor(name, shape, dt))

        def sem(name):
            return stack.enter_context(nc.semaphore(name))

        PROJ = [Wq2, Wk2, Wv2, Wk1, Wq1, Wv1]
        wgu = [sb("wgu_hi", [P, E, KT, 2, I], F32R), sb("wgu_lo", [P, E, KT, 2, I], F32R)]
        wdn_hi = sb("wdn_hi", [P, E, D], F32R)
        wgate = [sb("wgate_hi", [P, KT, E], F32R), sb("wgate_lo", [P, KT, E], F32R)]
        wout = sb("wout", [P, PAIRS, D])
        bias = sb("bias", [P, D])
        qT = [sb(f"qT{d}", [P, PAIRS, S]) for d in range(2)]
        kT = [sb(f"kT{d}", [P, PAIRS, S]) for d in range(2)]
        ident = sb("ident", [P, P])
        before = sb("before", [P, P], BF16)
        ones = sb("ones", [P, P], BF16)
        share = sb("share", [P, TT, TOP_K])
        al = sb("al", [P, 2])
        alphas = sb("alphas", [P, 2])
        mhalf = sb("mhalf", [P, ST])
        expert = sb("expert", [P, E])
        region = sb("region", [P, E])
        base = sb("base", [P, E])
        target = sb("target", [P, ST, TOP_K])
        table_row = sb("table_row", [1, 2, TC * P], I32)

        fills = sb("fills", [P, MOST])
        tri = sb("tri", [P, E, E])
        group_no = sb("group_no", [P, TC])

        with ExitStack() as a:
            wp = [sb("wp_hi", [P, 6, KT, INNER], F32R, a), sb("wp_lo", [P, 6, KT, INNER], F32R, a)]
            gate_rows = sb("gate_rows", [E, D], stack=a)
            val = [sb(f"val{d}", [P, ST, INNER], stack=a) for d in range(2)]
            rows = sb("rows", [P, ST, D], stack=a)
            rowsT = [sb("rowsT_hi", [P, KT, S], F32R, a), sb("rowsT_lo", [P, KT, S], F32R, a)]
            x_in = sb("x_in", [P, ST, D], stack=a)
            x_res = sb("x_res", [P, ST, D], stack=a)
            x_mid = sb("x_mid", [P, ST, D], stack=a)
            probs = [sb(f"probs{i}", [P, 2, ST, S], stack=a) for i in range(2)]
            probsT = sb("probsT", [P, 2, ST, S], stack=a)
            attnT = sb("attnT", [P, PAIRS, S], stack=a)
            moeT = [sb("moeT_hi", [P, KT, S], F32R, a), sb("moeT_lo", [P, KT, S], F32R, a)]
            routed = sb("routed", [P, ST, TOP_K, ROW], stack=a)
            pad_target = sb("pad_target", [P, 2 * E, 2], I32, a)
            small = lambda name, shape, dt=F32: sb(name, shape, dt, a)
            mx, nmx, sums, inv, rec = ([small(f"{n}{i}", [P, 4]) for i in range(2)]
                                       for n in ("mx", "nmx", "sums", "inv", "rec"))
            stats = small("stats", [P, ST, 6])
            mv = small("mv", [P, ST, 2])
            ve = small("ve", [P, ST])
            rstd = small("rstd", [P, ST])
            lmax = small("lmax", [P, ST])
            lexp = small("lexp", [P, ST, E])
            pexp = small("pexp", [P, ST, E])
            top = small("top", [P, ST, 8])
            topi = small("topi", [P, ST, 8], U32)
            topf = small("topf", [P, ST, TOP_K])
            tsum = small("tsum", [P, ST])
            trec = small("trec", [P, ST])
            onehot = small("onehot", [P, ST, TOP_K, E])
            chosen = small("chosen", [P, ST, E])
            chosen_b = small("chosen_b", [P, ST, E], BF16)
            place = small("place", [P, ST, E])
            slotf = small("slotf", [P, ST, TOP_K])
            slot_i = small("slot_i", [P, ST, TOP_K], I32)
        with ExitStack() as later:
            wdn_lo = sb("wdn_lo", [P, E, D], F32R, later)
            wdn = [wdn_hi, wdn_lo]
            xg = [sb(f"xg{i}", [P, 2, ROW], stack=later) for i in range(LOADS)]
            xgT = [[sb(f"xgT_hi{i}", [P, 2, KT, P], F32R, later), sb(f"xgT_lo{i}", [P, 2, KT, P], F32R, later)]
                   for i in range(2)]
            gated = [sb(f"gated{i}", [P, 2, I], stack=later) for i in range(2)]
            actT = [[sb(f"actT_hi{i}", [P, 2, P], F32R, later), sb(f"actT_lo{i}", [P, 2, P], F32R, later)]
                    for i in range(2)]
            y_out = [sb(f"y_out{i}", [P, 2, D], stack=later) for i in range(4)]
            plan = lambda name, shape, dt=F32: sb(name, shape, dt, later)
            count = plan("count", [P, E])
            over = plan("over", [P, E, MOST])
            ngroups = plan("ngroups", [P, E])
            trin = plan("trin", [P, E, E])
            ends = plan("ends", [P, E])
            past = plan("past", [P, TC, E])
            pastn = plan("pastn", [P, TC, E])
            texp = plan("texp", [P, TC])
            tstart = plan("tstart", [P, TC])
            trow = plan("trow", [P, TC])
            table = plan("table", [P, 2, TC], I32)
            base_i = plan("base_i", [P, E], I32)
        with ExitStack() as last:
            y_in = [sb(f"y_in{i}", [P, ST, TOP_K, D], stack=last) for i in range(4)]
            z = [sb(f"z{i}", [P, ST, D], stack=last) for i in range(4)]

        with ExitStack() as a:
            p_s = ps("p_s", [P, 4, 2 * S], stack=a)
            p_pt = ps("p_pt", [P, 2, 2 * S], stack=a)
            p_av = ps("p_av", [P, 2 * S], stack=a)
            p_x = ps("p_x", [P, 2 * S], stack=a)
        p_xt = ps("p_xt", [P, 2, 2, KT, P])
        p_gu = ps("p_gu", [P, 2, 2, 2 * I])
        p_at = ps("p_at", [P, 2, 512])
        p_y = ps("p_y", [P, 2, 2, D])

        sems = {}

        def new(*names):
            for n in names:
                sems[n] = sem(n)
            return [sems[n] for n in names] if len(names) > 1 else sems[names[0]]

        piece_in = [sem(f"piece_in{i}") for i in range(4)]
        const_in, x_landed, ctx_landed, mid_stored, rows_sent, pads_sent, first_pads = new(
            "const_in", "x_landed", "ctx_landed", "mid_stored", "rows_sent", "pads_sent", "first_pads")
        table_out, table_in = new("table_out", "table_in")
        xg_in = [sem(f"xg_in{i}") for i in range(LOADS)]
        y_sent = [sem(f"y_sent{i}") for i in range(4)]
        y_back = [sem(f"y_back{i}") for i in range(4)]
        out_stored = [sem(f"out_stored{i}") for i in range(4)]
        consts_set, al_set, piece_hi, piece_lo, gate_t, gate_hi, gate_lo = new(
            "consts_set", "al_set", "piece_hi", "piece_lo", "gate_t", "gate_hi", "gate_lo")
        ctx_t, x_t, rowsT_hi, rowsT_lo, proj_done, proj_out = new(
            "ctx_t", "x_t", "rowsT_hi_set", "rowsT_lo_set", "proj_done", "proj_out")
        scores_done, mx_set, nmx_set, exp_done, inv_set, rec_set, normed_p, normed_v = new(
            "scores_done", "mx_set", "nmx_set", "exp_done", "inv_set", "rec_set", "normed_p", "normed_v")
        pt_done, pt_out_a, pt_out_b, av_done, attn_out, outp_done, mid_set = new(
            "pt_done", "pt_out_a", "pt_out_b", "av_done", "attn_out", "outp_done", "mid_set")
        stats_set, mv_set, ve_set, rstd_set, ln1_set, ln2_set, x_res_set = new(
            "stats_set", "mv_set", "ve_set", "rstd_set", "ln1_set", "ln2_set", "x_res_set")
        moe_t, moeT_hi, moeT_lo, logits_done, logits_read, router_step, router_exp, places_done, copies_set = new(
            "moe_t", "moeT_hi_set", "moeT_lo_set", "logits_done", "logits_read", "router_step", "router_exp",
            "places_done", "copies_set")
        plan_step = new("plan_step")
        xg_t, xgT_hi, xgT_lo, gu_done, tanh_done, gate_step, act_set, act_t, actT_hi, actT_lo, down_done, y_set = new(
            "xg_t", "xgT_hi_set", "xgT_lo_set", "gu_done", "tanh_done", "gate_step", "act_set", "act_t",
            "actT_hi_set", "actT_lo_set", "down_done", "y_set")
        z_step = new("z_step")

        x_dram = x.rearrange("b (t p) d -> b p t d", p=P)
        ctx_dram = ctx.rearrange("b (t p) d -> b p t d", p=P)
        out_dram = out.rearrange("b (t p) d -> b p t d", p=P)
        mid_dram = mid_rows.rearrange("(b t p) d -> b p t d", t=ST, p=P)
        y_dram = y_rows[0:DUMP, :].rearrange("(b t p k) d -> b p t k d", t=ST, p=P, k=TOP_K)

        slot = [flat(t[:, :, :]) for t in (qT[0], kT[0], qT[1], kT[1])]
        pieces = []
        for n, w in enumerate(PROJ):
            pieces.append(([(slot[len(pieces) % 4].rearrange("p (k n) -> p k n", k=KT),
                             w.rearrange("(k p) n -> p k n", p=P))],
                           [flat(t[:, n, :, :]) for t in wp]))
        for e in range(0, E, 2):
            v = slot[len(pieces) % 4].rearrange("p (e k g i) -> p e k g i", e=2, k=KT, g=2)
            pieces.append(([(v[:, j, :, g, :], w[e + j].rearrange("(k p) i -> p k i", p=P))
                            for j in range(2) for g, w in enumerate((w1, w3))],
                           [flat(t[:, e:e + 2, :, :, :]) for t in wgu]))
        DOWN = E // 4
        for again in range(2):
            for e in range(0, E, 4):
                parts = [flat(wdn_hi[:, e:e + 4, :]), flat(wdn_lo[:, e:e + 4, :])]
                pieces.append(([(slot[len(pieces) % 4].rearrange("p (e n) -> p e n", e=4),
                                 w2[e:e + 4].rearrange("e p n -> p e n"))],
                               [None, parts[1]] if again else [parts[0], None]))
        EARLY = len(pieces) - DOWN

        def arrived(n):
            return 16 * sum(len(pieces[m][0]) for m in range(n % 4, n + 1, 4))

        def norm1(b):
            return 1 if isinstance(b, int) and b == 0 else 2 * b

        def norm2(b, cur):
            return 2 * b + 1 if cur else 2 * b

        N_CONST = 4
        block = stack.enter_context(nc.Block())

        def stage_a(eng, body):
            body(0, True, False)
            body(1, True, True)
            with eng.Fori(2, B) as b:
                body(b, True, True)
            body(B, False, True)

        def stage_b(eng, body, before=0, after=3):
            for j in range(-before, LOADS):
                body(j, j % LOADS)
            with eng.Fori(1, GROUPS // LOADS - 1) as q:
                for r in range(LOADS):
                    body(LOADS * q + r, r)
            for j in range(GROUPS - LOADS, GROUPS + after):
                body(j, j % LOADS)

        def exists(j):
            return not isinstance(j, int) or 0 <= j < GROUPS

        @block.sync
        def _(sp):
            sp.dma_start(rows[:, :, :], ctx_dram[0]).then_inc(ctx_landed, 16)
            sp.dma_start(x_in[:, :, :], x_dram[0]).then_inc(x_landed, 16)
            sp.dma_start(gate_rows[:, :], gate_w).then_inc(const_in, 16)
            sp.dma_start(wout[:, :, :], Wout.rearrange("(c p) n -> p c n", p=P)).then_inc(const_in, 16)
            sp.dma_start(bias[:, :], bout.rearrange("(a n) -> a n", a=1).to_broadcast([P, D])).then_inc(const_in, 16)
            sp.dma_start(al[:, 0:1], alpha_attn.rearrange("(a n) -> a n", a=1).to_broadcast([P, 1])).then_inc(const_in, 16)

            def load_piece(n):
                for dst, src in pieces[n][0]:
                    sp.dma_start(dst, src).then_inc(piece_in[n % 4], 16)

            for n in range(EARLY):
                if n >= 4:
                    sp.wait_ge(piece_hi, n - 3)
                    sp.wait_ge(piece_lo, min(n - 3, EARLY - DOWN))
                load_piece(n)

            def pad(row, n, groups, done):
                to = x_rows[bass.ds(row, groups * GROUP), :].rearrange("(n p) d -> p n d", p=P)
                sp.dma_start(to[:, :, 0:D], spread(bias[:, :], 1, [P, 2 * groups, D])).then_inc(done, 16)
                sp.dma_start(to[:, :, D:D + 1].bitcast(I32), flat(pad_target[:, n:n + groups, :]).unsqueeze(2),
                             allow_slow_non_contiguous=True).then_inc(done, 16)

            sp.wait_ge(const_in, 16 * N_CONST)
            sp.wait_ge(consts_set, 7)
            pad(E * REGION, E, E, pads_sent)

            def iteration(b, load, store):
                if load:
                    sp.wait_ge(x_t, b + 1)
                    sp.dma_start(rows[:, :, :], ctx_dram[b + 1]).then_inc(ctx_landed, 16)
                if store:
                    sp.wait_ge(mid_set, b)
                    sp.dma_start(mid_dram[b - 1], x_mid[:, :, :]).then_inc(mid_stored, 16)
                if load:
                    sp.wait_ge(ln1_set, b + 1)
                    sp.wait_ge(x_res_set, b + 1)
                    sp.dma_start(x_in[:, :, :], x_dram[b + 1]).then_inc(x_landed, 16)

            iteration(0, True, False)
            with sp.Fori(1, B - 1) as b:
                iteration(b, True, True)
            iteration(B - 1, False, True)
            sp.wait_ge(outp_done, B)
            for n in range(EARLY, EARLY + DOWN):
                load_piece(n)
            iteration(B, False, True)
            def pad_expert(e, done):
                pad(sp.value_load(base_i[0:1, e:e + 1], min_val=e * REGION, max_val=e * REGION + TOKENS), e, 1, done)

            EAGER = 4
            sp.wait_ge(plan_step, 13)
            for e in range(EAGER):
                pad_expert(e, first_pads)
            sp.wait_ge(plan_step, 15)
            sp.dma_start(tile_table.rearrange("v (c p) -> p v c", p=P), table[:, :, :],
                         allow_slow_non_contiguous=True).then_inc(table_out, 16)
            sp.wait_ge(table_out, 16)
            sp.dma_start(table_row[:, :, :], tile_table.rearrange("(a v) n -> a v n", a=1)).then_inc(table_in, 16)
            sp.wait_ge(rows_sent, 16 * ST * TOP_K * B)
            sp.wait_ge(first_pads, 32 * EAGER)
            sp.wait_ge(table_in, 16)

            def load_group(j, r):
                row = sp.value_load(table_row[0:1, 0, bass.ds(j, 1)], min_val=0, max_val=E * REGION + (E - 1) * GROUP)
                sp.dma_start(xg[r][:, :, 0:D + 1],
                             x_rows[bass.ds(row, GROUP), 0:D + 1].rearrange("(n p) d -> p n d", p=P)).then_inc(xg_in[r], 16)

            for r in range(EAGER):
                load_group(r, r)
            for e in range(EAGER, E):
                pad_expert(e, pads_sent)
            sp.wait_ge(pads_sent, 32 * (E - EAGER + 1))
            for r in range(EAGER, LOADS):
                load_group(r, r)
            with sp.Fori(1, GROUPS // LOADS) as q:
                for r in range(LOADS):
                    wait_alone(sp, xg_t, LOADS * (q - 1) + r + 1)
                    sp.wait_ge(y_sent[r % 4], 32 * (2 * q + r // 4 - 1))
                    load_group(LOADS * q + r, r)

            for i in range(4):
                sp.wait_ge(y_sent[i], 32 * (GROUPS // 4))
            sp.wait_ge(mid_stored, 16 * B)
            for r in range(4):
                sp.dma_start(y_in[r][:, :, :, :], y_dram[r]).then_inc(y_back[r], 16)
                sp.dma_start(z[r][:, :, :], mid_dram[r]).then_inc(y_back[r], 16)
            if B > 4:
                with sp.Fori(1, B // 4) as q:
                    for r in range(4):
                        sp.wait_ge(out_stored[r], 16 * q)
                        sp.dma_start(y_in[r][:, :, :, :], y_dram[4 * q + r]).then_inc(y_back[r], 16)
                        sp.dma_start(z[r][:, :, :], mid_dram[4 * q + r]).then_inc(y_back[r], 16)

        @block.gpsimd
        def _(pool):
            for t in (ident, before, ones, routed):
                v = t[tuple([slice(None)] * len(t.shape))]
                pool.memset(v, 1.0 if t is ones or t is before else 0.0).then_inc(consts_set, 1)
            pool.wait_ge(consts_set, 4)
            pool.affine_select(out=ident[:, :], in_=ident[:, :], compare_op=ALU.not_equal, fill=1.0,
                               base=0, pattern=[[-1, P]], channel_multiplier=1).then_inc(consts_set, 1)
            pool.affine_select(out=before[:, :], in_=before[:, :], compare_op=ALU.is_gt, fill=0.0,
                               base=0, pattern=[[1, P]], channel_multiplier=-1).then_inc(consts_set, 1)
            pool.iota(pad_target[:, :, :], [[GROUP, 2 * E], [P, 2]], base=DUMP, channel_multiplier=1).then_inc(consts_set, 1)
            pool.memset(mhalf[:, :], -0.5).then_inc(consts_set, 1)
            for t, pattern, start, mult in (
                    (expert[:, :], [[1, E]], 0, 0),
                    (region[:, :], [[REGION, E]], 0, 0),
                    (base[:, :], [[REGION, E]], 0, 0),
                    (target[:, :, :], [[P * TOP_K, ST], [1, TOP_K]], 0, TOP_K),
                    (fills[:, :], [[GROUP, MOST]], 0, 0),
                    (tri[:, :, :], [[1, E], [-1, E]], 0, 0),
                    (group_no[:, :], [[P, TC]], 0, 1)):
                pool.iota(t, pattern, base=start, channel_multiplier=mult,
                          allow_small_or_imprecise_dtypes=True).then_inc(consts_set, 1)
            pool.wait_ge(const_in, 16 * N_CONST)

            def rsqrt(n):
                pool.wait_ge(ve_set, n)
                pool.tensor_tensor(rstd[:, :], ve[:, :], mhalf[:, :], ALU.pow).then_inc(rstd_set, 1)

            def send(i):
                t, k = i // TOP_K, i % TOP_K
                pool.indirect_dma_start(x_rows, bass.IndirectOffsetOnAxis(ap=slot_i[:, t, k:k + 1], axis=0),
                                        routed[:, t, k, :], None).then_inc(rows_sent, 16)

            def normalise(b, u):
                pool.wait_ge(rec_set, STEPS * b + u + 1)
                pr, rc = probs[u % 2], rec[u % 2]
                pool.tensor_tensor(pr[:, 0, 0, :], pr[:, 0, 0, :], rc[:, 0:1].to_broadcast([P, S]),
                                   ALU.mult).then_inc(normed_p, 1)
                pool.tensor_scalar(pr[:, 0, 1, :], pr[:, 0, 1, :], rc[:, 1:2], None, ALU.mult).then_inc(normed_p, 1)

            def iteration(b, cur, prev):
                if cur:
                    rsqrt(norm1(b))
                if prev:
                    rsqrt(norm2(b, cur))
                if cur:
                    wait(pool, mid_set, b)
                    pool.wait_ge(x_landed, 16 * (b + 1))
                    pool.tensor_tensor(x_res[:, :, :], x_in[:, :, :], spread(bias[:, :], 1, [P, ST, D]),
                                       ALU.add).then_inc(x_res_set, 1)
                    for u in range(STEPS):
                        normalise(b, u)
                        if prev and u >= 2:
                            if u == 2:
                                wait_alone(pool, router_step, ROUTER_STEPS * b)
                                wait_alone(pool, copies_set, b)
                            for i in {6: (4, 5), 7: (6, 7)}.get(u, (u - 2,)):
                                send(i)
                elif prev:
                    pool.wait_ge(router_step, ROUTER_STEPS * b)
                    pool.wait_ge(copies_set, b)
                    for i in range(ST * TOP_K):
                        send(i)

            stage_a(pool, iteration)

            def return_group(j, r):
                if exists(j):
                    wait_alone(pool, y_set, j + 1)
                    for i in range(2):
                        pool.indirect_dma_start(
                            y_rows, bass.IndirectOffsetOnAxis(ap=xg[r][:, i, D:D + 1].bitcast(I32), axis=0),
                            y_out[r % 4][:, i, :], None).then_inc(y_sent[r % 4], 16)

            stage_b(pool, return_group, after=0)

        @block.scalar
        def _(act):
            act.wait_ge(const_in, 16 * N_CONST)
            act.activation(al[:, 1:2], al[:, 0:1], ACT.Tanh, scale=0.5).then_inc(al_set, 1)
            for n in range(EARLY):
                act.wait_ge(piece_in[n % 4], arrived(n))
                act.copy(pieces[n][1][0], slot[n % 4]).then_inc(piece_hi, 1)
            act.wait_ge(gate_t, 1)
            act.copy(flat(wgate[0][:, :, :]), p_x[:, 0:KT * E]).then_inc(gate_hi, 1)

            def proj_evac(b, n, dst):
                act.wait_ge(proj_done, PROJS * b + n + 1)
                if n == 0 and isinstance(b, int) and b == 0:
                    act.wait_ge(piece_lo, EARLY - DOWN)
                act.copy(dst, p_s[:, n % 4, :]).then_inc(proj_out, 1)

            def probsT_out(b, u):
                act.wait_ge(pt_done, 2 * (STEPS * b + u) + 1)
                wait(act, av_done, STEPS * b + u)
                act.copy(flat(probsT[:, 0, :, :]), p_pt[:, 0, :]).then_inc(pt_out_a, 1)

            def attn_evac(b, p):
                act.wait_ge(av_done, STEPS * b + 2 * p + 2)
                act.copy(attnT[:, p, :], p_av[:, 0:S]).then_inc(attn_out, 1)

            def exps(b, u):
                act.wait_ge(nmx_set, STEPS * b + u + 1)
                wait(act, pt_done, 2 * (STEPS * b + u - 1))
                wait(act, inv_set, STEPS * b + u - 1)
                for g in range(4):
                    h, t = g // 2, g % 2
                    act.activation(probs[u % 2][:, h, t, :], p_s[:, 2 * (u % 2) + h, t * S:(t + 1) * S], ACT.Exp,
                                   bias=nmx[u % 2][:, g:g + 1], scale=SCALE,
                                   accum_out=sums[u % 2][:, g:g + 1]).then_inc(exp_done, 1)

            def iteration(b, cur, prev):
                pb = b - 1
                if cur:
                    act.wait_ge(ctx_t, b + 1)
                    wait(act, proj_done, PROJS * b)
                    act.copy(flat(rowsT[0][:, :, :]), p_x[:, :]).then_inc(rowsT_hi, 1)
                if prev:
                    probsT_out(pb, STEPS - 2)
                    attn_evac(pb, PAIRS - 2)
                if cur:
                    proj_evac(b, 0, flat(qT[0][:, 0:2, :]))
                if prev:
                    probsT_out(pb, STEPS - 1)
                if cur:
                    proj_evac(b, 1, flat(qT[0][:, 2:4, :]))
                if prev:
                    attn_evac(pb, PAIRS - 1)
                if cur:
                    proj_evac(b, 2, flat(kT[1][:, 0:2, :]))
                    proj_evac(b, 3, flat(kT[1][:, 2:4, :]))
                    proj_evac(b, 4, val[1][:, 0, :])
                    proj_evac(b, 5, val[1][:, 1, :])
                    act.wait_ge(x_t, b + 1)
                    act.copy(flat(rowsT[0][:, :, :]), p_pt[:, 0, :]).then_inc(rowsT_hi, 1)
                    proj_evac(b, 6, flat(kT[0][:, 0:2, :]))
                    proj_evac(b, 7, flat(kT[0][:, 2:4, :]))
                    proj_evac(b, 8, flat(qT[1][:, 0:2, :]))
                if prev:
                    act.wait_ge(moe_t, pb + 1)
                    wait(act, logits_done, pb)
                    act.copy(flat(moeT[0][:, :, :]), p_pt[:, 1, :]).then_inc(moeT_hi, 1)
                if cur:
                    proj_evac(b, 9, flat(qT[1][:, 2:4, :]))
                    proj_evac(b, 10, val[0][:, 0, :])
                if prev:
                    act.wait_ge(logits_read, pb + 1)
                    wait(act, router_step, ROUTER_STEPS * pb)
                    act.activation(pexp[:, :, :], lexp[:, :, :], ACT.Exp).then_inc(router_exp, 1)
                if cur:
                    proj_evac(b, 11, val[0][:, 1, :])
                    for u in range(STEPS):
                        if u >= 2:
                            probsT_out(b, u - 2)
                        exps(b, u)
                        if u >= 4 and u % 2 == 0:
                            attn_evac(b, u // 2 - 2)

            stage_a(act, iteration)

            def group(j, r):
                if exists(j - 1):
                    i = (r + 1) % 2
                    act.wait_ge(gu_done, j)
                    wait(act, act_t, j - 2)
                    act.activation(gated[i][:, :, :], p_gu[:, i, :, 0:I], ACT.Tanh, scale=0.5).then_inc(tanh_done, 1)
                if exists(j - 2):
                    i = r % 2
                    act.wait_ge(act_t, j - 1)
                    wait(act, down_done, j - 3)
                    act.copy(flat(actT[i][0][:, :, :]), p_at[:, i, 0:2 * P]).then_inc(actT_hi, 1)
                if exists(j - 3):
                    i, o = (r + 1) % 2, (r + 1) % 4
                    act.wait_ge(down_done, j - 2)
                    wait(act, y_sent[o], 8 * (j - 3 - o))
                    act.copy(flat(y_out[o][:, :, :]), flat(p_y[:, i, :, :])).then_inc(y_set, 1)
                if exists(j + 1):
                    i = (r + 1) % 2
                    act.wait_ge(xg_t, j + 2)
                    wait(act, gu_done, j)
                    act.copy(flat(xgT[i][0][:, :, :, :]), flat(p_xt[:, i, :, :, :])).then_inc(xgT_hi, 1)

            stage_b(act, group, before=1, after=3)

            for r in range(4):
                act.wait_ge(z_step, ST * TOP_K * (r + 1))
                act.dma_start(out_dram[r], z[r][:, :, :]).then_inc(out_stored[r], 16)
            if B > 4:
                with act.Fori(1, B // 4) as q:
                    for r in range(4):
                        act.wait_ge(z_step, ST * TOP_K * (4 * q + r + 1))
                        act.dma_start(out_dram[4 * q + r], z[r][:, :, :]).then_inc(out_stored[r], 16)
            for r in range(4):
                act.wait_ge(out_stored[r], 16 * (B // 4))

        @block.vector
        def _(dve):
            dve.wait_ge(al_set, 1)
            dve.tensor_scalar(alphas[:, 0:1], al[:, 1:2], 0.5, 0.5, ALU.mult, ALU.add).then_inc(al_set, 1)
            dve.tensor_scalar(alphas[:, 1:2], al[:, 1:2], -0.5, 0.5, ALU.mult, ALU.add).then_inc(al_set, 1)
            for n in range(EARLY - DOWN):
                dve.wait_ge(piece_hi, n + 1)
                hi, lo = pieces[n][1]
                dve.tensor_tensor(lo, slot[n % 4], hi.bitcast(F32), ALU.subtract).then_inc(piece_lo, 1)
            dve.wait_ge(gate_hi, 1)
            dve.tensor_tensor(flat(wgate[1][:, :, :]), p_x[:, 0:KT * E], flat(wgate[0][:, :, :]).bitcast(F32),
                              ALU.subtract).then_inc(gate_lo, 1)
            dve.wait_ge(consts_set, 15)

            def probsT_out(b, u):
                dve.wait_ge(pt_done, 2 * (STEPS * b + u) + 2)
                wait(dve, av_done, STEPS * b + u)
                dve.tensor_copy(flat(probsT[:, 1, :, :]), p_pt[:, 1, :]).then_inc(pt_out_b, 1)

            def layer_norm(n, src, dst, done):
                for t in range(ST):
                    last = dve.bn_stats(stats[:, t, :], src[:, t, :])
                last.then_inc(stats_set, 1)
                wait_alone(dve, stats_set, n)
                for t in range(ST):
                    last = dve.bn_aggr(mv[:, t, :], stats[:, t, :])
                last.then_inc(mv_set, 1)
                dve.wait_ge(mv_set, n)
                dve.tensor_scalar(ve[:, :], mv[:, :, 1], EPS, None, ALU.add).then_inc(ve_set, 1)
                dve.wait_ge(rstd_set, n)
                for t in range(ST):
                    last = dve.tensor_scalar(dst(t), src[:, t, :], mv[:, t, 0:1], rstd[:, t:t + 1],
                                             ALU.subtract, ALU.mult)
                last.then_inc(done, 1)

            def router(m):
                step = ROUTER_STEPS * m
                TE = [P, ST, TOP_K, E]
                logits = p_x[:, 0:ST * E].rearrange("p (t e) -> p t e", t=ST)
                dve.wait_ge(logits_done, m + 1)
                dve.tensor_reduce(lmax[:, :], logits, AX.X, ALU.max).then_inc(router_step, 1)
                dve.wait_ge(router_step, step + 1)
                dve.tensor_tensor(lexp[:, :, :], logits, spread(lmax[:, :], 2, [P, ST, E]),
                                  ALU.subtract).then_inc(logits_read, 1)
                wait_alone(dve, router_exp, m + 1)
                for t in range(ST):
                    dve.max(top[:, t, :], pexp[:, t, :]).then_inc(router_step, 1)
                dve.wait_ge(router_step, step + 3)
                dve.tensor_reduce(tsum[:, :], top[:, :, 0:TOP_K], AX.X, ALU.add).then_inc(router_step, 1)
                for t in range(ST):
                    dve.max_index(topi[:, t, :], top[:, t, :], pexp[:, t, :]).then_inc(router_step, 1)
                dve.wait_ge(router_step, step + 6)
                dve.tensor_copy(topf[:, :, :], topi[:, :, 0:TOP_K]).then_inc(router_step, 1)
                dve.reciprocal(trec[:, :], tsum[:, :]).then_inc(router_step, 1)
                dve.wait_ge(router_step, step + 8)
                dve.tensor_tensor(onehot[:, :, :, :], spread(spread(expert[:, :], 1, [P, TOP_K, E]), 1, TE),
                                  spread(topf[:, :, :], 3, TE), ALU.is_equal).then_inc(router_step, 1)
                dve.scalar_tensor_tensor(share[:, bass.ds(ST * m, ST), :], top[:, :, 0:TOP_K], 0.5,
                                         spread(trec[:, :], 2, [P, ST, TOP_K]),
                                         ALU.mult, ALU.mult).then_inc(router_step, 1)
                dve.wait_ge(router_step, step + 10)
                dve.tensor_reduce(chosen[:, :, :], onehot[:, :, :, :].rearrange("p t k e -> p t e k"), AX.X,
                                  ALU.add).then_inc(router_step, 1)
                dve.wait_ge(router_step, step + 11)
                dve.tensor_copy(chosen_b[:, :, :], chosen[:, :, :]).then_inc(router_step, 1)

            def route(m):
                step = ROUTER_STEPS * m
                TE = [P, ST, TOP_K, E]
                dve.wait_ge(places_done, m + 1)
                dve.tensor_tensor(place[:, :, :], p_x[:, 64:64 + ST * E].rearrange("p (t e) -> p t e", t=ST),
                                  spread(base[:, :], 1, [P, ST, E]), ALU.add).then_inc(router_step, 1)
                dve.wait_ge(router_step, step + 13)
                dve.tensor_tensor(base[:, :], p_x[:, 96:96 + E], base[:, :], ALU.add).then_inc(router_step, 1)
                dve.tensor_tensor(onehot[:, :, :, :], onehot[:, :, :, :], spread(place[:, :, :], 2, TE),
                                  ALU.mult).then_inc(router_step, 1)
                dve.wait_ge(router_step, step + 15)
                dve.tensor_reduce(slotf[:, :, :], onehot[:, :, :, :], AX.X, ALU.add).then_inc(router_step, 1)
                dve.wait_ge(router_step, step + 16)
                wait(dve, rows_sent, 16 * ST * TOP_K * m)
                dve.tensor_copy(slot_i[:, :, :], slotf[:, :, :]).then_inc(router_step, 1)
                dve.tensor_copy(routed[:, :, :, D].bitcast(I32), target[:, :, :]).then_inc(router_step, 1)
                dve.wait_ge(router_step, step + 18)
                dve.tensor_scalar(target[:, :, :], target[:, :, :], float(S * TOP_K), None,
                                  ALU.add).then_inc(router_step, 1)

            def row_max(b, u):
                dve.wait_ge(scores_done, STEPS * b + u + 1)
                i = u % 2
                dve.tensor_reduce(mx[i][:, :], p_s[:, 2 * i:2 * i + 2, :].rearrange("p h (t k) -> p (h t) k", t=ST),
                                  AX.X, ALU.max).then_inc(mx_set, 1)
                dve.wait_ge(mx_set, STEPS * b + u + 1)
                wait(dve, exp_done, 4 * (STEPS * b + u - 1))
                dve.tensor_scalar(nmx[i][:, :], mx[i][:, :], -SCALE, None, ALU.mult).then_inc(nmx_set, 1)

            def normalise(b, u):
                i = u % 2
                dve.wait_ge(exp_done, 4 * (STEPS * b + u + 1))
                dve.reciprocal(inv[i][:, :], sums[i][:, :]).then_inc(inv_set, 1)
                dve.wait_ge(inv_set, STEPS * b + u + 1)
                wait(dve, normed_p, 2 * (STEPS * b + u - 1))
                dve.tensor_scalar(rec[i][:, :], inv[i][:, :], alphas[:, i:i + 1], None, ALU.mult).then_inc(rec_set, 1)
                dve.wait_ge(rec_set, STEPS * b + u + 1)
                for t in range(ST):
                    dve.tensor_scalar(probs[i][:, 1, t, :], probs[i][:, 1, t, :], rec[i][:, 2 + t:3 + t], None,
                                      ALU.mult).then_inc(normed_v, 1)

            def iteration(b, cur, prev):
                pb = b - 1
                if cur:
                    dve.wait_ge(rowsT_hi, 2 * b + 1)
                    wait(dve, proj_done, PROJS * b)
                    dve.tensor_tensor(flat(rowsT[1][:, :, :]), p_x[:, :],
                                      flat(rowsT[0][:, :, :]).bitcast(F32), ALU.subtract).then_inc(rowsT_lo, 1)
                if prev:
                    probsT_out(pb, STEPS - 2)
                    probsT_out(pb, STEPS - 1)
                if cur:
                    dve.wait_ge(x_landed, 16 * (b + 1))
                    dve.wait_ge(ctx_t, b + 1)
                    layer_norm(norm1(b), x_in, lambda t: rows[:, t, :], ln1_set)
                    dve.wait_ge(rowsT_hi, 2 * b + 2)
                    dve.wait_ge(proj_done, PROJS * b + 6)
                    dve.tensor_tensor(flat(rowsT[1][:, :, :]), p_pt[:, 0, :],
                                      flat(rowsT[0][:, :, :]).bitcast(F32), ALU.subtract).then_inc(rowsT_lo, 1)
                if prev:
                    dve.wait_ge(outp_done, pb + 1)
                    dve.wait_ge(x_res_set, pb + 1)
                    wait(dve, mid_stored, 16 * pb)
                    dve.tensor_tensor(flat(x_mid[:, :, :]), p_av[:, :], flat(x_res[:, :, :]),
                                      ALU.add).then_inc(mid_set, 1)
                    dve.wait_ge(mid_set, pb + 1)
                    wait(dve, rows_sent, 16 * ST * TOP_K * pb)
                    layer_norm(norm2(b, cur), x_mid, lambda t: routed[:, t, 0, 0:D], ln2_set)
                    dve.wait_ge(moeT_hi, pb + 1)
                    wait(dve, logits_done, pb)
                    dve.tensor_tensor(flat(moeT[1][:, :, :]), p_pt[:, 1, :],
                                      flat(moeT[0][:, :, :]).bitcast(F32), ALU.subtract).then_inc(moeT_lo, 1)
                    router(pb)
                if prev and not cur:
                    route(pb)
                for u in range(STEPS if cur else 0):
                    row_max(b, u)
                    if u:
                        normalise(b, u - 1)
                    if u >= 2:
                        probsT_out(b, u - 2)
                    if prev and u == 1:
                        route(pb)
                    if prev and u == 0:
                        copies(pb)
                if cur:
                    normalise(b, STEPS - 1)
                else:
                    copies(pb)

            def copies(m):
                dve.wait_ge(ln2_set, m + 1)
                for t in range(ST):
                    last = dve.tensor_copy(routed[:, t, 1:TOP_K, 0:D], spread(routed[:, t, 0, 0:D], 1, [P, TOP_K - 1, D]))
                last.then_inc(copies_set, 1)

            stage_a(dve, iteration)

            n_steps = [0]

            def planned(ins):
                n_steps[0] += 1
                ins.then_inc(plan_step, 1)
                dve.wait_ge(plan_step, n_steps[0])

            TE = [P, TC, E]
            dve.wait_ge(router_step, ROUTER_STEPS * B)
            planned(dve.tensor_tensor(count[:, :], base[:, :], region[:, :], ALU.subtract))
            planned(dve.tensor_tensor(over[:, :, :], spread(count[:, :], 2, [P, E, MOST]),
                                      spread(fills[:, :], 1, [P, E, MOST]), ALU.is_gt))
            planned(dve.tensor_reduce(ngroups[:, :], over[:, :, :], AX.X, ALU.add))
            planned(dve.tensor_scalar(tri[:, :, :], tri[:, :, :], 0.0, None, ALU.is_ge))
            planned(dve.tensor_tensor(trin[:, :, :], tri[:, :, :], spread(ngroups[:, :], 1, [P, E, E]), ALU.mult))
            planned(dve.tensor_reduce(ends[:, :], trin[:, :, :], AX.X, ALU.add))
            planned(dve.tensor_tensor(past[:, :, :], spread(group_no[:, :], 2, TE), spread(ends[:, :], 1, TE), ALU.is_ge))
            planned(dve.tensor_reduce(texp[:, :], past[:, :, :], AX.X, ALU.add))
            planned(dve.tensor_tensor(pastn[:, :, :], past[:, :, :], spread(ngroups[:, :], 1, TE), ALU.mult))
            planned(dve.tensor_reduce(tstart[:, :], pastn[:, :, :], AX.X, ALU.add))
            planned(dve.tensor_tensor(tstart[:, :], group_no[:, :], tstart[:, :], ALU.subtract))
            planned(dve.tensor_scalar(trow[:, :], texp[:, :], float(REGION), None, ALU.mult))
            planned(dve.tensor_copy(base_i[:, :], base[:, :]))
            planned(dve.scalar_tensor_tensor(trow[:, :], tstart[:, :], float(GROUP), trow[:, :], ALU.mult, ALU.add))
            dve.tensor_scalar(table[:, 1, :], texp[:, :], float(E - 1), None, ALU.min)
            planned(dve.tensor_copy(table[:, 0, :], trow[:, :]))
            for n in range(EARLY, EARLY + DOWN):
                dve.wait_ge(piece_in[n % 4], arrived(n))
                lo, e = pieces[n][1][1], 4 * (n - EARLY)
                dve.tensor_tensor(lo, slot[n % 4], flat(wdn_hi[:, e:e + 4, :]).bitcast(F32),
                                  ALU.subtract).then_inc(piece_lo, 1)

            def group(j, r):
                if exists(j - 1):
                    i = (r + 1) % 2
                    dve.wait_ge(tanh_done, j)
                    dve.scalar_tensor_tensor(gated[i][:, :, :], gated[i][:, :, :], 1.0, p_gu[:, i, :, 0:I],
                                             ALU.add, ALU.mult).then_inc(gate_step, 1)
                    dve.wait_ge(gate_step, j)
                    dve.tensor_tensor(gated[i][:, :, :], p_gu[:, i, :, I:2 * I], gated[i][:, :, :],
                                      ALU.mult).then_inc(act_set, 1)
                if exists(j - 2):
                    i = r % 2
                    dve.wait_ge(actT_hi, j - 1)
                    wait(dve, down_done, j - 3)
                    dve.tensor_tensor(flat(actT[i][1][:, :, :]), p_at[:, i, 0:2 * P],
                                      flat(actT[i][0][:, :, :]).bitcast(F32), ALU.subtract).then_inc(actT_lo, 1)
                if exists(j + 1):
                    i = (r + 1) % 2
                    dve.wait_ge(xgT_hi, j + 2)
                    wait(dve, gu_done, j)
                    dve.tensor_tensor(flat(xgT[i][1][:, :, :, :]), flat(p_xt[:, i, :, :, :]),
                                      flat(xgT[i][0][:, :, :, :]).bitcast(F32), ALU.subtract).then_inc(xgT_lo, 1)

            stage_b(dve, group, before=1, after=2)

            def total(b, r, loads):
                dve.wait_ge(y_back[r], loads)
                for k in range(TOP_K):
                    for t in range(ST):
                        if k:
                            dve.wait_ge(z_step, ST * TOP_K * b + ST * k + t - 1)
                        dve.scalar_tensor_tensor(z[r][:, t, :], y_in[r][:, t, k, :],
                                                 share[:, bass.ds(ST * b + t, 1), k], z[r][:, t, :],
                                                 ALU.mult, ALU.add).then_inc(z_step, 1)

            for r in range(4):
                total(r, r, 32)
            if B > 4:
                with dve.Fori(1, B // 4) as q:
                    for r in range(4):
                        total(4 * q + r, r, 32 * (q + 1))

        @block.tensor
        def _(pe):
            pe.wait_ge(consts_set, 15)
            pe.wait_ge(const_in, 16 * N_CONST)
            for k in range(KT):
                last = pe.transpose(p_x[:, k * E:(k + 1) * E], gate_rows[:, k * P:(k + 1) * P], ident[0:E, 0:E])
            last.then_inc(gate_t, 1)

            PASSES = ((0, 0), (0, 1), (1, 0))

            def transpose_rows(dst, src):
                for k in range(KT):
                    for t in range(ST):
                        mm = pe.transpose(dst[:, k * S + t * P:k * S + (t + 1) * P],
                                          src(t)[:, k * P:(k + 1) * P], ident[:, :])
                return mm

            def project_cols(n, w, pair0):
                for j in range(2):
                    c = (pair0 + j) * P
                    i = 0
                    for k in range(KT):
                        for a, r in PASSES:
                            mm = pe.matmul(p_s[:, n % 4, j * S:(j + 1) * S], wp[a][:, w, k, c:c + P], rowsT[r][:, k, :],
                                           start=(i == 0), stop=(i == 5))
                            i += 1
                mm.then_inc(proj_done, 1)

            def project_rows(n, w, t):
                i = 0
                for k in range(KT):
                    for r, a in PASSES:
                        mm = pe.matmul(p_s[:, n % 4, :], rowsT[r][:, k, t * P:(t + 1) * P], wp[a][:, w, k, :],
                                       start=(i == 0), stop=(i == 5))
                        i += 1
                mm.then_inc(proj_done, 1)

            def project(b, n):
                if n < 4:
                    wait(pe, exp_done, 4 * (STEPS * b - 1 + n // 2))
                else:
                    pe.wait_ge(proj_out, PROJS * b + n - 3)
                w = n // 2
                if w in (2, 5):
                    project_rows(n, w, n % 2)
                else:
                    project_cols(n, w, 2 * (n % 2))

            def scores(b, u):
                p, d = u // 2, u % 2
                if u < 2:
                    pe.wait_ge(proj_out, PROJS * b + 10 + 2 * u)
                else:
                    pe.wait_ge(exp_done, 4 * (STEPS * b + u - 1))
                for t in range(ST):
                    for h in range(2):
                        r = HEAD_DIM * h
                        mm = pe.matmul(p_s[:, 2 * d + h, t * S:(t + 1) * S],
                                       qT[d][r:r + HEAD_DIM, p, t * P:(t + 1) * P],
                                       kT[d][r:r + HEAD_DIM, p, :], start=True, stop=True)
                mm.then_inc(scores_done, 1)

            def probs_t(b, u):
                pe.wait_ge(normed_p, 2 * (STEPS * b + u + 1))
                pe.wait_ge(normed_v, 2 * (STEPS * b + u + 1))
                if u == 0:
                    pe.wait_ge(rowsT_lo, 2 * b + 2)
                    wait(pe, moeT_lo, b)
                else:
                    pe.wait_ge(pt_out_a, STEPS * b + u)
                    pe.wait_ge(pt_out_b, STEPS * b + u)
                for h in range(2):
                    for k in range(ST):
                        for t in range(ST):
                            mm = pe.transpose(p_pt[:, h, k * S + t * P:k * S + (t + 1) * P],
                                              probs[u % 2][:, h, t, k * P:(k + 1) * P], ident[:, :])
                    mm.then_inc(pt_done, 1)

            def attend(b, u):
                p, d = u // 2, u % 2
                pe.wait_ge(pt_out_a, STEPS * b + u + 1)
                pe.wait_ge(pt_out_b, STEPS * b + u + 1)
                if d == 0 and p:
                    pe.wait_ge(attn_out, PAIRS * b + p)
                if u == 0:
                    wait(pe, mid_set, b)
                for k in range(ST):
                    for h in range(2):
                        r = HEAD_DIM * h
                        c = p * P + r
                        mm = pe.matmul(p_av[r:r + HEAD_DIM, 0:S], val[d][:, k, c:c + HEAD_DIM], probsT[:, h, k, :],
                                       start=(d == 0 and k == 0), stop=(d == 1 and k == ST - 1),
                                       skip_group_check=True)
                mm.then_inc(av_done, 1)

            def out_project(b):
                pe.wait_ge(attn_out, PAIRS * (b + 1))
                for t in range(ST):
                    for c in range(PAIRS):
                        mm = pe.matmul(p_av[:, t * D:(t + 1) * D], attnT[:, c, t * P:(t + 1) * P], wout[:, c, :],
                                       start=(c == 0), stop=(c == PAIRS - 1))
                mm.then_inc(outp_done, 1)

            def logits(m):
                pe.wait_ge(moeT_lo, m + 1)
                for t in range(ST):
                    n = 0
                    for k in range(KT):
                        for r, a in PASSES:
                            mm = pe.matmul(p_x[:, t * E:(t + 1) * E], moeT[r][:, k, t * P:(t + 1) * P],
                                           wgate[a][:, k, :], start=(n == 0), stop=(n == 5))
                            n += 1
                mm.then_inc(logits_done, 1)

            def places(m):
                pe.wait_ge(router_step, ROUTER_STEPS * m + 12)
                pe.matmul(p_x[:, 64:64 + E], before[:, :], chosen_b[:, 0, :], start=True, stop=True)
                pe.matmul(p_x[:, 64 + E:64 + 2 * E], before[:, :], chosen_b[:, 1, :], start=True, stop=False)
                pe.matmul(p_x[:, 64 + E:64 + 2 * E], ones[:, :], chosen_b[:, 0, :], start=False, stop=True)
                pe.matmul(p_x[:, 96:96 + E], ones[:, :], chosen_b[:, 0, :], start=True, stop=False)
                pe.matmul(p_x[:, 96:96 + E], ones[:, :], chosen_b[:, 1, :], start=False,
                          stop=True).then_inc(places_done, 1)

            def iteration(b, cur, prev):
                pb = b - 1
                if cur:
                    pe.wait_ge(ctx_landed, 16 * (b + 1))
                    wait(pe, router_step, ROUTER_STEPS * (b - 1))
                    if isinstance(b, int) and b == 0:
                        pe.wait_ge(gate_lo, 1)
                    transpose_rows(p_x, lambda t: rows[:, t, :]).then_inc(ctx_t, 1)
                if prev:
                    probs_t(pb, STEPS - 2)
                    attend(pb, STEPS - 3)
                if cur:
                    pe.wait_ge(rowsT_lo, 2 * b + 1)
                    if isinstance(b, int) and b == 0:
                        pe.wait_ge(piece_lo, 6)
                    project(b, 0)
                if prev:
                    attend(pb, STEPS - 2)
                    probs_t(pb, STEPS - 1)
                if cur:
                    project(b, 1)
                if prev:
                    attend(pb, STEPS - 1)
                if cur:
                    for n in range(2, 6):
                        project(b, n)
                    pe.wait_ge(ln1_set, b + 1)
                    wait(pe, pt_out_a, STEPS * b)
                    transpose_rows(p_pt[:, 0, :], lambda t: rows[:, t, :]).then_inc(x_t, 1)
                if prev:
                    out_project(pb)
                if cur:
                    pe.wait_ge(rowsT_lo, 2 * b + 2)
                    for n in range(6, 9):
                        project(b, n)
                if prev:
                    pe.wait_ge(ln2_set, pb + 1)
                    pe.wait_ge(pt_out_b, STEPS * b)
                    transpose_rows(p_pt[:, 1, :], lambda t: routed[:, t, 0, 0:D]).then_inc(moe_t, 1)
                if cur:
                    project(b, 9)
                    project(b, 10)
                if prev:
                    logits(pb)
                if cur:
                    project(b, 11)
                    for u in range(STEPS):
                        scores(b, u)
                        if prev and u == 1:
                            places(pb)
                        if u >= 3:
                            attend(b, u - 3)
                        if u >= 2:
                            probs_t(b, u - 2)
                else:
                    places(pb)

            stage_a(pe, iteration)

            pe.wait_ge(table_in, 16)
            pe.wait_ge(piece_lo, EARLY)

            def expert_of(j):
                return pe.value_load(table_row[0:1, 1, bass.ds(j, 1)], min_val=0, max_val=E - 1)

            experts = {}

            def group(j, r):
                if exists(j - 2) and r < 2:
                    experts[(r - 2) % LOADS] = expert_of(j - 2)
                if exists(j + 1):
                    i = (r + 1) % 2
                    pe.wait_ge(xg_in[(r + 1) % LOADS], xg_loads(j + 1, r + 1))
                    wait(pe, xgT_lo, j)
                    for n in range(2):
                        for k in range(KT):
                            mm = pe.transpose(p_xt[:, i, n, k, :], xg[(r + 1) % LOADS][:, n, k * P:(k + 1) * P], ident[:, :])
                    mm.then_inc(xg_t, 1)
                if exists(j):
                    i = r % 2
                    experts[r] = expert_of(j)
                    pe.wait_ge(xgT_lo, j + 1)
                    wait(pe, act_set, j - 1)
                    for n in range(2):
                        m = 0
                        for k in range(KT):
                            for h, a in PASSES:
                                mm = pe.matmul(p_gu[:, i, n, :], xgT[i][h][:, n, k, :],
                                               wgu[a][:, bass.ds(experts[r], 1), k, :, :].rearrange("p e g i -> p (e g i)"),
                                               start=(m == 0), stop=(m == 5))
                                m += 1
                    mm.then_inc(gu_done, 1)
                if exists(j - 1):
                    i = (r + 1) % 2
                    pe.wait_ge(act_set, j)
                    wait(pe, actT_lo, j - 2)
                    for n in range(2):
                        mm = pe.transpose(p_at[:, i, n * P:(n + 1) * P], gated[i][:, n, :], ident[:, :])
                    mm.then_inc(act_t, 1)
                if exists(j - 2):
                    i = r % 2
                    pe.wait_ge(actT_lo, j - 1)
                    wait(pe, y_set, j - 3)
                    for n in range(2):
                        for m, (h, a) in enumerate(PASSES):
                            mm = pe.matmul(p_y[:, i, n, :], actT[i][h][:, n, :],
                                           wdn[a][:, bass.ds(experts[(r - 2) % LOADS], 1), :].rearrange("p e d -> p (e d)"),
                                           start=(m == 0), stop=(m == 2))
                    mm.then_inc(down_done, 1)

            def xg_loads(j, r):
                return 16 // LOADS * (j - r % LOADS) + 16

            stage_b(pe, group, before=1, after=2)


_INS = ['x', 'ctx_1024', 'L0_xattn_Wq1', 'L0_xattn_Wk1', 'L0_xattn_Wv1', 'L0_xattn_Wq2', 'L0_xattn_Wk2',
        'L0_xattn_Wv2', 'L0_xattn_alpha_attn', 'L0_xattn_Wout', 'L0_xattn_bout', 'L0_ffn_gate_w', 'L0_ffn_w1',
        'L0_ffn_w3', 'L0_ffn_w2']


def kernel(**inputs):
    import numpy as _np
    import concourse.bacc as _bacc
    from concourse import mybir as _mybir
    from concourse.bass_utils import run_bass_kernel_spmd as _run

    nc = _bacc.Bacc("TRN2", target_bir_lowering=False, num_devices=1)
    arrays, args = {}, []
    for name in _INS:
        a = _np.ascontiguousarray(inputs[name])
        arrays[f"in_{name}_dram"] = a
        args.append(nc.dram_tensor(f"in_{name}_dram", a.shape, _mybir.dt.from_np(a.dtype), kind="ExternalInput").ap())
    shape = _np.shape(inputs["x"])
    args.append(nc.dram_tensor("out_0_dram", shape, _mybir.dt.float32, kind="ExternalOutput").ap())
    xattn_moe_kernel(nc, *args)
    r = _run(nc, [arrays], core_ids=[0])
    return r.results[0]["out_0_dram"]
```

```python
from contextlib import ExitStack

import concourse.bass as bass
from concourse import mybir

F32 = mybir.dt.float32
F32R = mybir.dt.float32r
U32 = mybir.dt.uint32
I32 = mybir.dt.int32
BF16 = mybir.dt.bfloat16
ALU = mybir.AluOpType
ACT = mybir.ActivationFunctionType
AX = mybir.AxisListType

P = 128
TOP_K = 4
EPS = 1e-5
HEAD_DIM = 64


def wait_alone(eng, sem, count):
    eng.wait_ge(sem, count)
    eng.nop(nofuse=True)


def flat(ap):
    names = " ".join("abcd"[:len(ap.shape) - 1])
    return ap.rearrange(f"p {names} -> p ({names})")


def spread(ap, axis, shape):
    return ap.unsqueeze(axis).to_broadcast(shape)


def wait(eng, sem, count):
    if isinstance(count, int) and count <= 0:
        return
    eng.wait_ge(sem, count)


def xattn_moe_kernel(nc, x, ctx, Wq1, Wk1, Wv1, Wq2, Wk2, Wv2, alpha_attn, Wout, bout,
                     gate_w, w1, w3, w2, out):
    B, S, D = x.shape
    INNER = Wq1.shape[1]
    E, _, I = w1.shape
    KT = D // P
    ST = S // P
    PAIRS = INNER // P
    STEPS = 2 * PAIRS
    PROJS = 6 * INNER * KT // 512
    SCALE = HEAD_DIM ** -0.5
    TOKENS = B * S
    TT = TOKENS // P
    GROUP = 2 * P
    REGION = TOKENS + GROUP
    ROW = D + 4
    GROUPS = TOKENS * TOP_K // GROUP + E
    MOST = TOKENS // GROUP
    DUMP = TOKENS * TOP_K
    PIECE = KT * INNER
    LOADS = 8
    TC = -(-GROUPS // P)
    assert S == 2 * P and D == 2 * P and INNER == 4 * P and I == P and B >= 4 and B % 4 == 0
    assert GROUPS % LOADS == 0 and GROUPS >= 3 * LOADS
    ROUTER_STEPS = 19

    x_rows = nc.dram_tensor("x_rows", [E * REGION + E * GROUP, ROW], F32, kind="Internal").ap()
    y_rows = nc.dram_tensor("y_rows", [DUMP + 2 * E * GROUP, D], F32, kind="Internal").ap()
    mid_rows = nc.dram_tensor("mid_rows", [TOKENS, D], F32, kind="Internal").ap()
    group_table = nc.dram_tensor("group_table", [2, TC * P], I32, kind="Internal").ap()

    with ExitStack() as stack:
        def sb(name, shape, dt=F32, stack=stack):
            return stack.enter_context(nc.sbuf_tensor(name, shape, dt))

        def ps(name, shape, dt=F32, stack=stack):
            return stack.enter_context(nc.psum_tensor(name, shape, dt))

        def sem(name):
            return stack.enter_context(nc.semaphore(name))

        PROJ = [Wq2, Wk2, Wv2, Wk1, Wq1, Wv1]
        wgu_hi = sb("wgu_hi", [P, E, KT, 2, I], F32R)
        wdn_hi = sb("wdn_hi", [P, E, D], F32R)
        wgate = [sb("wgate_hi", [P, KT, E], F32R), sb("wgate_lo", [P, KT, E], F32R)]
        wout = sb("wout", [P, PAIRS, D])
        bias = sb("bias", [P, D])
        ident = sb("ident", [P, P])
        before = sb("before", [P, P], BF16)
        ones = sb("ones", [P, P], BF16)
        share = sb("share", [P, TT, TOP_K])
        al = sb("al", [P, 2])
        alphas = sb("alphas", [P, 2])
        mhalf = sb("mhalf", [P, ST])
        expert = sb("expert", [P, E])
        region = sb("region", [P, E])
        base = sb("base", [P, E])
        target = sb("target", [P, ST, TOP_K])
        table_row = sb("table_row", [1, 2, TC * P], I32)

        fills = sb("fills", [P, MOST])
        tri = sb("tri", [P, E, E])
        group_no = sb("group_no", [P, TC])

        with ExitStack() as a:
            qT = [[sb(f"qT{d}_{part}", [P, PAIRS, S], F32R, a) for part in ("hi", "lo")] for d in range(2)]
            kT = [[sb(f"kT{d}_{part}", [P, PAIRS, S], F32R, a) for part in ("hi", "lo")] for d in range(2)]
            wp = [sb("wp_hi", [P, 6, KT, INNER], F32R, a), sb("wp_lo", [P, 6, KT, INNER], F32R, a)]
            gate_rows = sb("gate_rows", [E, D], stack=a)
            val = [sb(f"val{d}", [P, ST, INNER], stack=a) for d in range(2)]
            rows = sb("rows", [P, ST, D], stack=a)
            rowsT = [[sb(f"rowsT{i}_{part}", [P, KT, S], F32R, a) for part in ("hi", "lo")] for i in range(2)]
            x_in = sb("x_in", [P, ST, D], stack=a)
            x_res = sb("x_res", [P, ST, D], stack=a)
            x_mid = sb("x_mid", [P, ST, D], stack=a)
            probs = [sb(f"probs{i}", [P, 2, ST, S], stack=a) for i in range(2)]
            probsT = sb("probsT", [P, 2, ST, S], stack=a)
            attnT = sb("attnT", [P, PAIRS, S], stack=a)
            moeT = [sb("moeT_hi", [P, KT, S], F32R, a), sb("moeT_lo", [P, KT, S], F32R, a)]
            routed = sb("routed", [P, ST, TOP_K, ROW], stack=a)
            middle_slots = [sb(f"middle_slot{i}", [P, PIECE], stack=a)[:, :] for i in range(2)]
            pad_target = sb("pad_target", [P, 2 * E, 2], I32, a)
            small = lambda name, shape, dt=F32: sb(name, shape, dt, a)
            mx, nmx, sums, inv, rec = ([small(f"{n}{i}", [P, 4]) for i in range(2)]
                                       for n in ("mx", "nmx", "sums", "inv", "rec"))
            stats = small("stats", [P, ST, 6])
            mv = small("mv", [P, ST, 2])
            ve = small("ve", [P, ST])
            rstd = small("rstd", [P, ST])
            lmax = small("lmax", [P, ST])
            lexp = small("lexp", [P, ST, E])
            pexp = small("pexp", [P, ST, E])
            top = small("top", [P, ST, 8])
            topi = small("topi", [P, ST, 8], U32)
            topf = small("topf", [P, ST, TOP_K])
            tsum = small("tsum", [P, ST])
            trec = small("trec", [P, ST])
            onehot = small("onehot", [P, ST, TOP_K, E])
            chosen = small("chosen", [P, ST, E])
            chosen_b = small("chosen_b", [P, ST, E], BF16)
            place = small("place", [P, ST, E])
            slotf = small("slotf", [P, ST, TOP_K])
            slot_i = small("slot_i", [P, ST, TOP_K], I32)
        with ExitStack() as later:
            late_slots = [sb(f"late_slot{i}", [P, PIECE], stack=later)[:, :] for i in range(E // 2 + E // 4)]
            wgu_lo = sb("wgu_lo", [P, E, KT, 2, I], F32R, later)
            wdn_lo = sb("wdn_lo", [P, E, D], F32R, later)
            wgu = [wgu_hi, wgu_lo]
            wdn = [wdn_hi, wdn_lo]
            xg = [sb(f"xg{i}", [P, 2, ROW], stack=later) for i in range(LOADS)]
            xgT = [[sb(f"xgT_hi{i}", [P, 2, KT, P], F32R, later), sb(f"xgT_lo{i}", [P, 2, KT, P], F32R, later)]
                   for i in range(2)]
            gated = [sb(f"gated{i}", [P, 2, I], stack=later) for i in range(2)]
            actT = [[sb(f"actT_hi{i}", [P, 2, P], F32R, later), sb(f"actT_lo{i}", [P, 2, P], F32R, later)]
                    for i in range(2)]
            y_out = [sb(f"y_out{i}", [P, 2, D], stack=later) for i in range(4)]
            plan = lambda name, shape, dt=F32: sb(name, shape, dt, later)
            count = plan("count", [P, E])
            over = plan("over", [P, E, MOST])
            ngroups = plan("ngroups", [P, E])
            trin = plan("trin", [P, E, E])
            ends = plan("ends", [P, E])
            past = plan("past", [P, TC, E])
            pastn = plan("pastn", [P, TC, E])
            texp = plan("texp", [P, TC])
            tstart = plan("tstart", [P, TC])
            trow = plan("trow", [P, TC])
            table = plan("table", [P, 2, TC], I32)
            base_i = plan("base_i", [P, E], I32)
        with ExitStack() as last:
            y_in = [sb(f"y_in{i}", [P, ST, TOP_K, D], stack=last) for i in range(4)]
            z = [sb(f"z{i}", [P, ST, D], stack=last) for i in range(4)]

        with ExitStack() as a:
            p_s = ps("p_s", [P, 4, 2 * S], stack=a)
            p_pt = ps("p_pt", [P, 2, 2 * S], stack=a)
            p_av = ps("p_av", [P, 2 * S], stack=a)
            p_x = ps("p_x", [P, 2 * S], stack=a)
        p_xt = ps("p_xt", [P, 2, 2, KT, P])
        p_gu = ps("p_gu", [P, 2, 2, 2 * I])
        p_at = ps("p_at", [P, 2, 512])
        p_y = ps("p_y", [P, 2, 2, D])

        sems = {}

        def new(*names):
            for n in names:
                sems[n] = sem(n)
            return [sems[n] for n in names] if len(names) > 1 else sems[names[0]]

        LATE_SLOTS = len(late_slots)
        early_in = [sem(f"early_in{i}") for i in range(4)]
        middle_in = [sem(f"middle_in{i}") for i in range(2)]
        late_in = [sem(f"late_in{i}") for i in range(LATE_SLOTS)]
        wout_in = new("wout_in")
        const_in, x_landed, ctx_landed, mid_stored, rows_sent, pads_sent = new(
            "const_in", "x_landed", "ctx_landed", "mid_stored", "rows_sent", "pads_sent")
        table_out, table_in = new("table_out", "table_in")
        xg_in = [sem(f"xg_in{i}") for i in range(LOADS)]
        y_sent = [sem(f"y_sent{i}") for i in range(4)]
        y_back = [sem(f"y_back{i}") for i in range(4)]
        out_stored = [sem(f"out_stored{i}") for i in range(4)]
        consts_set, al_set, early_hi, early_lo, middle_hi, late_lo, gate_t, gate_hi, gate_lo = new(
            "consts_set", "al_set", "early_hi", "early_lo", "middle_hi", "late_lo", "gate_t", "gate_hi", "gate_lo")
        ctx_t, x_t, rowsT_hi, rowsT_lo, proj_done, proj_out = new(
            "ctx_t", "x_t", "rowsT_hi_set", "rowsT_lo_set", "proj_done", "proj_out")
        proj_lo = new("proj_lo")
        scores_done, mx_set, nmx_set, exp_done, inv_set, rec_set, normed_p, normed_v = new(
            "scores_done", "mx_set", "nmx_set", "exp_done", "inv_set", "rec_set", "normed_p", "normed_v")
        pt_done, pt_out_a, pt_out_b, av_done, attn_out, outp_done, mid_set = new(
            "pt_done", "pt_out_a", "pt_out_b", "av_done", "attn_out", "outp_done", "mid_set")
        stats_set, mv_set, ve_set, rstd_set, ln1_set, ln2_set, x_res_set = new(
            "stats_set", "mv_set", "ve_set", "rstd_set", "ln1_set", "ln2_set", "x_res_set")
        moe_t, moeT_hi, moeT_lo, logits_done, logits_read, router_step, router_exp, places_done, copies_set = new(
            "moe_t", "moeT_hi_set", "moeT_lo_set", "logits_done", "logits_read", "router_step", "router_exp",
            "places_done", "copies_set")
        plan_step = new("plan_step")
        xg_t, xgT_hi, xgT_lo, gu_done, tanh_done, gate_step, act_set, act_t, actT_hi, actT_lo, down_done, y_set = new(
            "xg_t", "xgT_hi_set", "xgT_lo_set", "gu_done", "tanh_done", "gate_step", "act_set", "act_t",
            "actT_hi_set", "actT_lo_set", "down_done", "y_set")
        z_step = new("z_step")

        x_dram = x.rearrange("b (t p) d -> b p t d", p=P)
        ctx_dram = ctx.rearrange("b (t p) d -> b p t d", p=P)
        out_dram = out.rearrange("b (t p) d -> b p t d", p=P)
        mid_dram = mid_rows.rearrange("(b t p) d -> b p t d", t=ST, p=P)
        y_dram = y_rows[0:DUMP, :].rearrange("(b t p k) d -> b p t k d", t=ST, p=P, k=TOP_K)

        early_slots = [flat(t) for t in (probs[0][:, :, :, :], probs[1][:, :, :, :], probsT[:, :, :, :], attnT[:, :, :])]

        def gate_up_source(e, slot):
            v = slot.rearrange("p (e k g i) -> p e k g i", e=2, k=KT, g=2)
            return [(v[:, :, :, g, :], w[e:e + 2].rearrange("e (k p) i -> p e k i", p=P))
                    for g, w in enumerate((w1, w3))]

        def down_source(e, slot):
            return [(slot.rearrange("p (e n) -> p e n", e=4), w2[e:e + 4].rearrange("e p n -> p e n"))]

        EARLY = len(PROJ)
        early = []
        for n, w in enumerate(PROJ):
            v = early_slots[n % 4]
            early.append((v, [(v.rearrange("p (k n) -> p k n", k=KT), w.rearrange("(k p) n -> p k n", p=P))],
                          flat(wp[0][:, n, :, :]), flat(wp[1][:, n, :, :])))
        middle = []
        for e in range(0, E, 2):
            v = middle_slots[len(middle) % 2]
            middle.append((v, gate_up_source(e, v), flat(wgu_hi[:, e:e + 2, :, :, :])))
        for e in range(0, E, 4):
            v = middle_slots[len(middle) % 2]
            middle.append((v, down_source(e, v), flat(wdn_hi[:, e:e + 4, :])))
        MIDDLE = len(middle)
        late = []
        for e in range(0, E, 2):
            v = late_slots[len(late)]
            late.append((v, gate_up_source(e, v), flat(wgu_hi[:, e:e + 2, :, :, :]), flat(wgu_lo[:, e:e + 2, :, :, :])))
        for e in range(0, E, 4):
            v = late_slots[len(late)]
            late.append((v, down_source(e, v), flat(wdn_hi[:, e:e + 4, :]), flat(wdn_lo[:, e:e + 4, :])))
        LATE = len(late)

        def arrived(pieces, slots, n):
            return 16 * sum(len(pieces[m][1]) for m in range(n % slots, n + 1, slots))

        def norm1(b):
            return 1 if isinstance(b, int) and b == 0 else 2 * b

        def norm2(b, cur):
            return 2 * b + 1 if cur else 2 * b

        N_CONST = 3
        EARLY_BEFORE = {0: (0, 1, 2), 1: (3,), 2: (4,), 3: (5,)}
        MIDDLE_BEFORE = {0: {5: 0, 6: 1, 10: 2, 11: 3}, 1: {3: 8, 4: 9, 8: 10, 9: 11}}
        MIDDLE_STEPS = {2: 4, 3: 5, 5: 6, 6: 7}
        assert EARLY == 6 and MIDDLE == 12 and STEPS == 8

        def proj_bank(n):
            if n < 8:
                return p_s[:, n % 4, :]
            return (p_s[:, 2, :], p_s[:, 3, :], p_av[:, :], p_pt[:, 0, :])[n - 8]

        block = stack.enter_context(nc.Block())

        def stage_a(eng, body):
            body(0, True, False, True)
            body(1, True, True, True)
            with eng.Fori(2, B - 1) as b:
                body(b, True, True, True)
            body(B - 1, True, True, False)
            body(B, False, True, False)

        def stage_b(eng, body, before=0, after=3):
            for j in range(-before, LOADS):
                body(j, j % LOADS)
            with eng.Fori(1, GROUPS // LOADS - 1) as q:
                for r in range(LOADS):
                    body(LOADS * q + r, r)
            for j in range(GROUPS - LOADS, GROUPS + after):
                body(j, j % LOADS)

        def exists(j):
            return not isinstance(j, int) or 0 <= j < GROUPS

        def pad(eng, row, n, groups):
            to = x_rows[bass.ds(row, groups * GROUP), :].rearrange("(n p) d -> p n d", p=P)
            eng.dma_start(to[:, :, 0:D], spread(bias[:, :], 1, [P, 2 * groups, D])).then_inc(pads_sent, 16)
            eng.dma_start(to[:, :, D:D + 1].bitcast(I32), flat(pad_target[:, n:n + groups, :]).unsqueeze(2),
                          allow_slow_non_contiguous=True).then_inc(pads_sent, 16)

        def pad_experts(eng, experts):
            for e in experts:
                row = eng.value_load(base_i[0:1, e:e + 1], min_val=e * REGION, max_val=e * REGION + TOKENS)
                pad(eng, row, e, 1)

        @block.sync
        def _(sp):
            sp.dma_start(rows[:, :, :], ctx_dram[0]).then_inc(ctx_landed, 16)
            sp.dma_start(gate_rows[:, :], gate_w).then_inc(const_in, 16)
            sp.dma_start(bias[:, :], bout.rearrange("(a n) -> a n", a=1).to_broadcast([P, D])).then_inc(const_in, 16)
            sp.dma_start(al[:, 0:1], alpha_attn.rearrange("(a n) -> a n", a=1).to_broadcast([P, 1])).then_inc(const_in, 16)

            def load_piece(pieces, n, arrivals):
                for dst, src in pieces[n][1]:
                    sp.dma_start(dst, src).then_inc(arrivals[n % len(arrivals)], 16)

            for n in range(EARLY):
                if n >= 4:
                    sp.wait_ge(early_lo, n - 3)
                load_piece(early, n, early_in)
            sp.dma_start(wout[:, :, :], Wout.rearrange("(c p) n -> p c n", p=P)).then_inc(wout_in, 16)
            sp.dma_start(x_in[:, :, :], x_dram[0]).then_inc(x_landed, 16)
            for n in range(2):
                load_piece(middle, n, middle_in)

            def iteration(b, load, store):
                if load:
                    sp.wait_ge(x_t, b + 1)
                    sp.dma_start(rows[:, :, :], ctx_dram[b + 1]).then_inc(ctx_landed, 16)
                if store:
                    sp.wait_ge(mid_set, b)
                    sp.dma_start(mid_dram[b - 1], x_mid[:, :, :]).then_inc(mid_stored, 16)
                if load:
                    sp.wait_ge(ln1_set, b + 1)
                    sp.wait_ge(x_res_set, b + 1)
                    sp.dma_start(x_in[:, :, :], x_dram[b + 1]).then_inc(x_landed, 16)

            iteration(0, True, False)
            for n in range(2, MIDDLE):
                sp.wait_ge(middle_hi, n - 1)
                load_piece(middle, n, middle_in)
            sp.wait_ge(const_in, 16 * N_CONST)
            sp.wait_ge(consts_set, 7)
            pad(sp, E * REGION, E, E)
            with sp.Fori(1, B - 1) as b:
                iteration(b, True, True)
            iteration(B - 1, False, True)
            sp.wait_ge(outp_done, B)
            for n in range(LATE):
                load_piece(late, n, late_in)
            iteration(B, False, True)
            sp.wait_ge(plan_step, 15)
            sp.dma_start(group_table.rearrange("v (c p) -> p v c", p=P), table[:, :, :],
                         allow_slow_non_contiguous=True).then_inc(table_out, 16)
            pad_experts(sp, range(0, E, 2))
            sp.wait_ge(table_out, 16)
            sp.dma_start(table_row[:, :, :], group_table.rearrange("(a v) n -> a v n", a=1)).then_inc(table_in, 16)
            sp.wait_ge(rows_sent, 16 * ST * TOP_K * B)
            sp.wait_ge(pads_sent, 32 * (E + 1))
            sp.wait_ge(table_in, 16)

            def load_group(j, r):
                row = sp.value_load(table_row[0:1, 0, bass.ds(j, 1)], min_val=0, max_val=E * REGION + (E - 1) * GROUP)
                sp.dma_start(xg[r][:, :, 0:D + 1],
                             x_rows[bass.ds(row, GROUP), 0:D + 1].rearrange("(n p) d -> p n d", p=P)).then_inc(xg_in[r], 16)

            for r in range(LOADS):
                load_group(r, r)
            with sp.Fori(1, GROUPS // LOADS) as q:
                for r in range(LOADS):
                    wait_alone(sp, xg_t, LOADS * (q - 1) + r + 1)
                    sp.wait_ge(y_sent[r % 4], 32 * (2 * q + r // 4 - 1))
                    load_group(LOADS * q + r, r)

            for i in range(4):
                sp.wait_ge(y_sent[i], 32 * (GROUPS // 4))
            sp.wait_ge(mid_stored, 16 * B)
            for r in range(4):
                sp.dma_start(y_in[r][:, :, :, :], y_dram[r]).then_inc(y_back[r], 16)
                sp.dma_start(z[r][:, :, :], mid_dram[r]).then_inc(y_back[r], 16)
            if B > 4:
                with sp.Fori(1, B // 4) as q:
                    for r in range(4):
                        sp.wait_ge(out_stored[r], 16 * q)
                        sp.dma_start(y_in[r][:, :, :, :], y_dram[4 * q + r]).then_inc(y_back[r], 16)
                        sp.dma_start(z[r][:, :, :], mid_dram[4 * q + r]).then_inc(y_back[r], 16)

        @block.gpsimd
        def _(pool):
            for t in (ident, before, ones, routed):
                v = t[tuple([slice(None)] * len(t.shape))]
                pool.memset(v, 1.0 if t is ones or t is before else 0.0).then_inc(consts_set, 1)
            pool.wait_ge(consts_set, 4)
            pool.affine_select(out=ident[:, :], in_=ident[:, :], compare_op=ALU.not_equal, fill=1.0,
                               base=0, pattern=[[-1, P]], channel_multiplier=1).then_inc(consts_set, 1)
            pool.affine_select(out=before[:, :], in_=before[:, :], compare_op=ALU.is_gt, fill=0.0,
                               base=0, pattern=[[1, P]], channel_multiplier=-1).then_inc(consts_set, 1)
            pool.iota(pad_target[:, :, :], [[GROUP, 2 * E], [P, 2]], base=DUMP, channel_multiplier=1).then_inc(consts_set, 1)
            pool.memset(mhalf[:, :], -0.5).then_inc(consts_set, 1)
            for t, pattern, start, mult in (
                    (expert[:, :], [[1, E]], 0, 0),
                    (region[:, :], [[REGION, E]], 0, 0),
                    (base[:, :], [[REGION, E]], 0, 0),
                    (target[:, :, :], [[P * TOP_K, ST], [1, TOP_K]], 0, TOP_K),
                    (fills[:, :], [[GROUP, MOST]], 0, 0),
                    (tri[:, :, :], [[1, E], [-1, E]], 0, 0),
                    (group_no[:, :], [[P, TC]], 0, 1)):
                pool.iota(t, pattern, base=start, channel_multiplier=mult,
                          allow_small_or_imprecise_dtypes=True).then_inc(consts_set, 1)
            pool.wait_ge(const_in, 16 * N_CONST)

            def rsqrt(n):
                pool.wait_ge(ve_set, n)
                pool.tensor_tensor(rstd[:, :], ve[:, :], mhalf[:, :], ALU.pow).then_inc(rstd_set, 1)

            def send(i):
                t, k = i // TOP_K, i % TOP_K
                pool.indirect_dma_start(x_rows, bass.IndirectOffsetOnAxis(ap=slot_i[:, t, k:k + 1], axis=0),
                                        routed[:, t, k, :], None).then_inc(rows_sent, 16)

            def normalise(b, u):
                pool.wait_ge(rec_set, STEPS * b + u + 1)
                pr, rc = probs[u % 2], rec[u % 2]
                for h, t in ((0, 0), (0, 1), (1, 0)):
                    g = 2 * h + t
                    pool.tensor_tensor(pr[:, h, t, :], pr[:, h, t, :], rc[:, g:g + 1].to_broadcast([P, S]),
                                       ALU.mult).then_inc(normed_p, 1)

            def iteration(b, cur, prev, following):
                if cur:
                    rsqrt(norm1(b))
                if prev and not (isinstance(b, int) and b == 1):
                    for i in range(2, ST * TOP_K):
                        send(i)
                if prev:
                    rsqrt(norm2(b, cur))
                if cur:
                    wait(pool, mid_set, b)
                    pool.wait_ge(x_landed, 16 * (b + 1))
                    pool.tensor_tensor(x_res[:, :, :], x_in[:, :, :], spread(bias[:, :], 1, [P, ST, D]),
                                       ALU.add).then_inc(x_res_set, 1)
                    for u in range(STEPS):
                        normalise(b, u)
                        if prev and u >= STEPS - 2:
                            if u == STEPS - 2:
                                wait_alone(pool, router_step, ROUTER_STEPS * b)
                                wait_alone(pool, copies_set, b)
                            send(u - (STEPS - 2))
                elif prev:
                    pool.wait_ge(router_step, ROUTER_STEPS * b)
                    pool.wait_ge(copies_set, b)
                    for i in range(ST * TOP_K):
                        send(i)

            stage_a(pool, iteration)

            def return_group(j, r):
                if exists(j):
                    wait_alone(pool, y_set, j + 1)
                    for i in range(2):
                        pool.indirect_dma_start(
                            y_rows, bass.IndirectOffsetOnAxis(ap=xg[r][:, i, D:D + 1].bitcast(I32), axis=0),
                            y_out[r % 4][:, i, :], None).then_inc(y_sent[r % 4], 16)

            stage_b(pool, return_group, after=0)

        @block.scalar
        def _(act):
            act.wait_ge(const_in, 16 * N_CONST)
            act.activation(al[:, 1:2], al[:, 0:1], ACT.Tanh, scale=0.5).then_inc(al_set, 1)
            act.wait_ge(gate_t, 1)
            act.copy(flat(wgate[0][:, :, :]), p_x[:, 0:KT * E]).then_inc(gate_hi, 1)

            def early_piece(n):
                act.wait_ge(early_in[n % 4], arrived(early, 4, n))
                act.copy(early[n][2], early[n][0]).then_inc(early_hi, 1)

            def middle_piece(n):
                act.wait_ge(middle_in[n % 2], arrived(middle, 2, n))
                act.copy(middle[n][2], middle[n][0]).then_inc(middle_hi, 1)

            def proj_evac(b, n, dst):
                if isinstance(b, int) and b == 0:
                    for m in EARLY_BEFORE.get(n, ()):
                        early_piece(m)
                if isinstance(b, int) and n in MIDDLE_BEFORE.get(b, ()):
                    middle_piece(MIDDLE_BEFORE[b][n])
                act.wait_ge(proj_done, PROJS * b + n + 1)
                act.copy(dst, proj_bank(n)).then_inc(proj_out, 1)

            def probsT_out(b, u):
                act.wait_ge(pt_done, 2 * (STEPS * b + u) + 1)
                wait(act, av_done, STEPS * b + u)
                act.copy(flat(probsT[:, 0, :, :]), p_pt[:, 0, :]).then_inc(pt_out_a, 1)

            def attn_evac(b, p):
                act.wait_ge(av_done, STEPS * b + 2 * p + 2)
                act.copy(attnT[:, p, :], p_av[:, 0:S]).then_inc(attn_out, 1)

            def exps(b, u):
                act.wait_ge(nmx_set, STEPS * b + u + 1)
                wait(act, pt_done, 2 * (STEPS * b + u - 1))
                wait(act, inv_set, STEPS * b + u - 1)
                for g in range(4):
                    h, t = g // 2, g % 2
                    act.activation(probs[u % 2][:, h, t, :], p_s[:, 2 * (u % 2) + h, t * S:(t + 1) * S], ACT.Exp,
                                   bias=nmx[u % 2][:, g:g + 1], scale=SCALE,
                                   accum_out=sums[u % 2][:, g:g + 1]).then_inc(exp_done, 1)

            def iteration(b, cur, prev, following):
                pb = b - 1
                if cur:
                    if isinstance(b, int) and b == 0:
                        context_hi(0)
                    proj_evac(b, 0, flat(qT[0][0][:, 0:2, :]))
                if prev:
                    attn_evac(pb, PAIRS - 2)
                    probsT_out(pb, STEPS - 2)
                if cur:
                    proj_evac(b, 1, flat(qT[0][0][:, 2:4, :]))
                    proj_evac(b, 2, flat(kT[1][0][:, 0:2, :]))
                if prev:
                    probsT_out(pb, STEPS - 1)
                if cur:
                    proj_evac(b, 3, flat(kT[1][0][:, 2:4, :]))
                if prev:
                    attn_evac(pb, PAIRS - 1)
                if cur:
                    act.wait_ge(x_t, b + 1)
                    act.copy(flat(rowsT[1][0][:, :, :]), p_pt[:, 0, :]).then_inc(rowsT_hi, 1)
                    proj_evac(b, 4, val[1][:, 0, :])
                    proj_evac(b, 5, val[1][:, 1, :])
                    proj_evac(b, 6, flat(kT[0][0][:, 0:2, :]))
                if prev:
                    act.wait_ge(moe_t, pb + 1)
                    wait(act, logits_done, pb)
                    act.copy(flat(moeT[0][:, :, :]), p_pt[:, 1, :]).then_inc(moeT_hi, 1)
                if cur:
                    proj_evac(b, 7, flat(kT[0][0][:, 2:4, :]))
                if prev:
                    act.wait_ge(logits_read, pb + 1)
                    wait(act, router_step, ROUTER_STEPS * pb)
                    act.activation(pexp[:, :, :], lexp[:, :, :], ACT.Exp).then_inc(router_exp, 1)
                if cur:
                    exps(b, 0)
                    proj_evac(b, 8, flat(qT[1][0][:, 0:2, :]))
                    proj_evac(b, 9, flat(qT[1][0][:, 2:4, :]))
                    proj_evac(b, 10, val[0][:, 0, :])
                    proj_evac(b, 11, val[0][:, 1, :])
                    exps(b, 1)
                    for u in range(2, STEPS):
                        if u >= 4 and u % 2 == 0:
                            attn_evac(b, u // 2 - 2)
                        if following and u == 6:
                            context_hi(b + 1)
                        probsT_out(b, u - 2)
                        exps(b, u)
                        if prev and u in (3, 4):
                            copies(pb, u - 3)
                        if isinstance(b, int) and b == 0 and u in MIDDLE_STEPS:
                            middle_piece(MIDDLE_STEPS[u])
                else:
                    for t in range(ST):
                        copies(pb, t)

            def context_hi(b):
                act.wait_ge(ctx_t, b + 1)
                act.copy(flat(rowsT[0][0][:, :, :]), p_x[:, :]).then_inc(rowsT_hi, 1)

            def copies(m, t):
                act.wait_ge(ln2_set, m + 1)
                ins = act.copy(routed[:, t, 1:TOP_K, 0:D], spread(routed[:, t, 0, 0:D], 1, [P, TOP_K - 1, D]))
                if t == ST - 1:
                    ins.then_inc(copies_set, 1)

            stage_a(act, iteration)
            act.wait_ge(plan_step, 15)
            pad_experts(act, range(1, E, 2))

            def group(j, r):
                if exists(j - 1):
                    i = (r + 1) % 2
                    act.wait_ge(gu_done, j)
                    wait(act, act_t, j - 2)
                    act.activation(gated[i][:, :, :], p_gu[:, i, :, 0:I], ACT.Tanh, scale=0.5).then_inc(tanh_done, 1)
                if exists(j - 2):
                    i = r % 2
                    act.wait_ge(act_t, j - 1)
                    wait(act, down_done, j - 3)
                    act.copy(flat(actT[i][0][:, :, :]), p_at[:, i, 0:2 * P]).then_inc(actT_hi, 1)
                if exists(j - 3):
                    i, o = (r + 1) % 2, (r + 1) % 4
                    act.wait_ge(down_done, j - 2)
                    wait(act, y_sent[o], 8 * (j - 3 - o))
                    act.copy(flat(y_out[o][:, :, :]), flat(p_y[:, i, :, :])).then_inc(y_set, 1)
                if exists(j + 1):
                    i = (r + 1) % 2
                    act.wait_ge(xg_t, j + 2)
                    wait(act, gu_done, j)
                    act.copy(flat(xgT[i][0][:, :, :, :]), flat(p_xt[:, i, :, :, :])).then_inc(xgT_hi, 1)

            stage_b(act, group, before=1, after=3)

            for r in range(4):
                act.wait_ge(z_step, ST * TOP_K * (r + 1))
                act.dma_start(out_dram[r], z[r][:, :, :]).then_inc(out_stored[r], 16)
            if B > 4:
                with act.Fori(1, B // 4) as q:
                    for r in range(4):
                        act.wait_ge(z_step, ST * TOP_K * (4 * q + r + 1))
                        act.dma_start(out_dram[4 * q + r], z[r][:, :, :]).then_inc(out_stored[r], 16)
            for r in range(4):
                act.wait_ge(out_stored[r], 16 * (B // 4))

        @block.vector
        def _(dve):
            dve.wait_ge(al_set, 1)
            dve.tensor_scalar(alphas[:, 0:1], al[:, 1:2], 0.5, 0.5, ALU.mult, ALU.add).then_inc(al_set, 1)
            dve.tensor_scalar(alphas[:, 1:2], al[:, 1:2], -0.5, 0.5, ALU.mult, ALU.add).then_inc(al_set, 1)
            dve.wait_ge(gate_hi, 1)
            dve.tensor_tensor(flat(wgate[1][:, :, :]), p_x[:, 0:KT * E], flat(wgate[0][:, :, :]).bitcast(F32),
                              ALU.subtract).then_inc(gate_lo, 1)
            dve.wait_ge(consts_set, 15)

            def probsT_out(b, u):
                dve.wait_ge(pt_done, 2 * (STEPS * b + u) + 2)
                wait(dve, av_done, STEPS * b + u)
                dve.tensor_copy(flat(probsT[:, 1, :, :]), p_pt[:, 1, :]).then_inc(pt_out_b, 1)

            def layer_norm(n, src, dst, done):
                for t in range(ST):
                    last = dve.bn_stats(stats[:, t, :], src[:, t, :])
                last.then_inc(stats_set, 1)
                wait_alone(dve, stats_set, n)
                for t in range(ST):
                    last = dve.bn_aggr(mv[:, t, :], stats[:, t, :])
                last.then_inc(mv_set, 1)
                dve.wait_ge(mv_set, n)
                dve.tensor_scalar(ve[:, :], mv[:, :, 1], EPS, None, ALU.add).then_inc(ve_set, 1)
                dve.wait_ge(rstd_set, n)
                for t in range(ST):
                    last = dve.tensor_scalar(dst(t), src[:, t, :], mv[:, t, 0:1], rstd[:, t:t + 1],
                                             ALU.subtract, ALU.mult)
                last.then_inc(done, 1)

            def read_logits(m):
                step = ROUTER_STEPS * m
                logits = p_x[:, 0:ST * E].rearrange("p (t e) -> p t e", t=ST)
                dve.wait_ge(logits_done, m + 1)
                dve.tensor_reduce(lmax[:, :], logits, AX.X, ALU.max).then_inc(router_step, 1)
                dve.wait_ge(router_step, step + 1)
                dve.tensor_tensor(lexp[:, :, :], logits, spread(lmax[:, :], 2, [P, ST, E]),
                                  ALU.subtract).then_inc(logits_read, 1)

            def router(m):
                step = ROUTER_STEPS * m
                TE = [P, ST, TOP_K, E]
                wait_alone(dve, router_exp, m + 1)
                for t in range(ST):
                    dve.max(top[:, t, :], pexp[:, t, :]).then_inc(router_step, 1)
                dve.wait_ge(router_step, step + 3)
                dve.tensor_reduce(tsum[:, :], top[:, :, 0:TOP_K], AX.X, ALU.add).then_inc(router_step, 1)
                for t in range(ST):
                    dve.max_index(topi[:, t, :], top[:, t, :], pexp[:, t, :]).then_inc(router_step, 1)
                dve.wait_ge(router_step, step + 6)
                dve.tensor_copy(topf[:, :, :], topi[:, :, 0:TOP_K]).then_inc(router_step, 1)
                dve.reciprocal(trec[:, :], tsum[:, :]).then_inc(router_step, 1)
                dve.wait_ge(router_step, step + 8)
                dve.tensor_tensor(onehot[:, :, :, :], spread(spread(expert[:, :], 1, [P, TOP_K, E]), 1, TE),
                                  spread(topf[:, :, :], 3, TE), ALU.is_equal).then_inc(router_step, 1)
                dve.scalar_tensor_tensor(share[:, bass.ds(ST * m, ST), :], top[:, :, 0:TOP_K], 0.5,
                                         spread(trec[:, :], 2, [P, ST, TOP_K]),
                                         ALU.mult, ALU.mult).then_inc(router_step, 1)
                dve.wait_ge(router_step, step + 10)
                dve.tensor_reduce(chosen[:, :, :], onehot[:, :, :, :].rearrange("p t k e -> p t e k"), AX.X,
                                  ALU.add).then_inc(router_step, 1)
                dve.wait_ge(router_step, step + 11)
                dve.tensor_copy(chosen_b[:, :, :], chosen[:, :, :]).then_inc(router_step, 1)

            def route(m):
                step = ROUTER_STEPS * m
                TE = [P, ST, TOP_K, E]
                dve.wait_ge(places_done, m + 1)
                dve.tensor_tensor(place[:, :, :], p_x[:, 64:64 + ST * E].rearrange("p (t e) -> p t e", t=ST),
                                  spread(base[:, :], 1, [P, ST, E]), ALU.add).then_inc(router_step, 1)
                dve.wait_ge(router_step, step + 13)
                dve.tensor_tensor(base[:, :], p_x[:, 96:96 + E], base[:, :], ALU.add).then_inc(router_step, 1)
                dve.tensor_tensor(onehot[:, :, :, :], onehot[:, :, :, :], spread(place[:, :, :], 2, TE),
                                  ALU.mult).then_inc(router_step, 1)
                dve.wait_ge(router_step, step + 15)
                dve.tensor_reduce(slotf[:, :, :], onehot[:, :, :, :], AX.X, ALU.add).then_inc(router_step, 1)
                dve.wait_ge(router_step, step + 16)
                wait(dve, rows_sent, 16 * ST * TOP_K * m)
                dve.tensor_copy(slot_i[:, :, :], slotf[:, :, :]).then_inc(router_step, 1)
                dve.tensor_copy(routed[:, :, :, D].bitcast(I32), target[:, :, :]).then_inc(router_step, 1)
                dve.wait_ge(router_step, step + 18)
                dve.tensor_scalar(target[:, :, :], target[:, :, :], float(S * TOP_K), None,
                                  ALU.add).then_inc(router_step, 1)

            def row_max(b, u):
                dve.wait_ge(scores_done, STEPS * b + u + 1)
                i = u % 2
                dve.tensor_reduce(mx[i][:, :], p_s[:, 2 * i:2 * i + 2, :].rearrange("p h (t k) -> p (h t) k", t=ST),
                                  AX.X, ALU.max).then_inc(mx_set, 1)
                dve.wait_ge(mx_set, STEPS * b + u + 1)
                wait(dve, exp_done, 4 * (STEPS * b + u - 1))
                dve.tensor_scalar(nmx[i][:, :], mx[i][:, :], -SCALE, None, ALU.mult).then_inc(nmx_set, 1)

            def normalise(b, u):
                i = u % 2
                dve.wait_ge(exp_done, 4 * (STEPS * b + u + 1))
                dve.reciprocal(inv[i][:, :], sums[i][:, :]).then_inc(inv_set, 1)
                dve.wait_ge(inv_set, STEPS * b + u + 1)
                wait(dve, normed_p, 3 * (STEPS * b + u - 1))
                dve.tensor_scalar(rec[i][:, :], inv[i][:, :], alphas[:, i:i + 1], None, ALU.mult).then_inc(rec_set, 1)
                dve.wait_ge(rec_set, STEPS * b + u + 1)
                dve.tensor_scalar(probs[i][:, 1, 1, :], probs[i][:, 1, 1, :], rec[i][:, 3:4], None,
                                  ALU.mult).then_inc(normed_v, 1)

            def context_lo(b):
                dve.wait_ge(rowsT_hi, 2 * b + 1)
                dve.tensor_tensor(flat(rowsT[0][1][:, :, :]), p_x[:, :],
                                  flat(rowsT[0][0][:, :, :]).bitcast(F32), ALU.subtract).then_inc(rowsT_lo, 1)

            def proj_rest(b, n, dst):
                if isinstance(b, int) and b == 0:
                    for m in EARLY_BEFORE.get(n, ()):
                        dve.wait_ge(early_hi, m + 1)
                        slot, _, hi, lo = early[m]
                        dve.tensor_tensor(lo, slot, hi.bitcast(F32), ALU.subtract).then_inc(early_lo, 1)
                dve.wait_ge(proj_out, PROJS * b + n + 1)
                dve.tensor_tensor(flat(dst[1]), proj_bank(n), flat(dst[0]).bitcast(F32), ALU.subtract).then_inc(proj_lo, 1)

            def half(parts, i):
                return [t[:, 2 * i:2 * i + 2, :] for t in parts]

            def iteration(b, cur, prev, following):
                pb = b - 1
                if cur:
                    if isinstance(b, int) and b == 0:
                        context_lo(0)
                    proj_rest(b, 0, half(qT[0], 0))
                if prev:
                    probsT_out(pb, STEPS - 2)
                if cur:
                    dve.wait_ge(x_landed, 16 * (b + 1))
                    dve.wait_ge(ctx_t, b + 1)
                    layer_norm(norm1(b), x_in, lambda t: rows[:, t, :], ln1_set)
                    proj_rest(b, 1, half(qT[0], 1))
                    proj_rest(b, 2, half(kT[1], 0))
                if prev:
                    probsT_out(pb, STEPS - 1)
                if cur:
                    proj_rest(b, 3, half(kT[1], 1))
                    dve.wait_ge(rowsT_hi, 2 * b + 2)
                    dve.tensor_tensor(flat(rowsT[1][1][:, :, :]), p_pt[:, 0, :],
                                      flat(rowsT[1][0][:, :, :]).bitcast(F32), ALU.subtract).then_inc(rowsT_lo, 1)
                if prev:
                    dve.wait_ge(outp_done, pb + 1)
                    dve.wait_ge(x_res_set, pb + 1)
                    wait(dve, mid_stored, 16 * pb)
                    dve.tensor_tensor(flat(x_mid[:, :, :]), p_av[:, :], flat(x_res[:, :, :]),
                                      ALU.add).then_inc(mid_set, 1)
                    dve.wait_ge(mid_set, pb + 1)
                    wait(dve, rows_sent, 16 * ST * TOP_K * pb)
                    layer_norm(norm2(b, cur), x_mid, lambda t: routed[:, t, 0, 0:D], ln2_set)
                if cur:
                    proj_rest(b, 6, half(kT[0], 0))
                if prev:
                    dve.wait_ge(moeT_hi, pb + 1)
                    dve.tensor_tensor(flat(moeT[1][:, :, :]), p_pt[:, 1, :],
                                      flat(moeT[0][:, :, :]).bitcast(F32), ALU.subtract).then_inc(moeT_lo, 1)
                if cur:
                    proj_rest(b, 7, half(kT[0], 1))
                if prev:
                    read_logits(pb)
                if cur:
                    row_max(b, 0)
                if prev:
                    router(pb)
                if cur:
                    proj_rest(b, 8, half(qT[1], 0))
                    proj_rest(b, 9, half(qT[1], 1))
                    normalise(b, 0)
                    row_max(b, 1)
                if cur:
                    for u in range(2, STEPS):
                        row_max(b, u)
                        normalise(b, u - 1)
                        probsT_out(b, u - 2)
                        if prev and u == 4:
                            route(pb)
                        if following and u == 6:
                            context_lo(b + 1)
                    normalise(b, STEPS - 1)
                else:
                    route(pb)

            stage_a(dve, iteration)

            n_steps = [0]

            def planned(ins):
                n_steps[0] += 1
                ins.then_inc(plan_step, 1)
                dve.wait_ge(plan_step, n_steps[0])

            TE = [P, TC, E]
            dve.wait_ge(router_step, ROUTER_STEPS * B)
            planned(dve.tensor_tensor(count[:, :], base[:, :], region[:, :], ALU.subtract))
            planned(dve.tensor_tensor(over[:, :, :], spread(count[:, :], 2, [P, E, MOST]),
                                      spread(fills[:, :], 1, [P, E, MOST]), ALU.is_gt))
            planned(dve.tensor_reduce(ngroups[:, :], over[:, :, :], AX.X, ALU.add))
            planned(dve.tensor_scalar(tri[:, :, :], tri[:, :, :], 0.0, None, ALU.is_ge))
            planned(dve.tensor_tensor(trin[:, :, :], tri[:, :, :], spread(ngroups[:, :], 1, [P, E, E]), ALU.mult))
            planned(dve.tensor_reduce(ends[:, :], trin[:, :, :], AX.X, ALU.add))
            planned(dve.tensor_tensor(past[:, :, :], spread(group_no[:, :], 2, TE), spread(ends[:, :], 1, TE), ALU.is_ge))
            planned(dve.tensor_reduce(texp[:, :], past[:, :, :], AX.X, ALU.add))
            planned(dve.tensor_tensor(pastn[:, :, :], past[:, :, :], spread(ngroups[:, :], 1, TE), ALU.mult))
            planned(dve.tensor_reduce(tstart[:, :], pastn[:, :, :], AX.X, ALU.add))
            planned(dve.tensor_tensor(tstart[:, :], group_no[:, :], tstart[:, :], ALU.subtract))
            planned(dve.tensor_scalar(trow[:, :], texp[:, :], float(REGION), None, ALU.mult))
            planned(dve.tensor_copy(base_i[:, :], base[:, :]))
            planned(dve.scalar_tensor_tensor(trow[:, :], tstart[:, :], float(GROUP), trow[:, :], ALU.mult, ALU.add))
            dve.tensor_scalar(table[:, 1, :], texp[:, :], float(E - 1), None, ALU.min)
            planned(dve.tensor_copy(table[:, 0, :], trow[:, :]))

            for n in range(LATE):
                dve.wait_ge(late_in[n], arrived(late, LATE_SLOTS, n))
                slot, _, hi, lo = late[n]
                dve.tensor_tensor(lo, slot, hi.bitcast(F32), ALU.subtract).then_inc(late_lo, 1)

            def group(j, r):
                if exists(j - 1):
                    i = (r + 1) % 2
                    dve.wait_ge(tanh_done, j)
                    dve.scalar_tensor_tensor(gated[i][:, :, :], gated[i][:, :, :], 1.0, p_gu[:, i, :, 0:I],
                                             ALU.add, ALU.mult).then_inc(gate_step, 1)
                    dve.wait_ge(gate_step, j)
                    dve.tensor_tensor(gated[i][:, :, :], p_gu[:, i, :, I:2 * I], gated[i][:, :, :],
                                      ALU.mult).then_inc(act_set, 1)
                if exists(j - 2):
                    i = r % 2
                    dve.wait_ge(actT_hi, j - 1)
                    wait(dve, down_done, j - 3)
                    dve.tensor_tensor(flat(actT[i][1][:, :, :]), p_at[:, i, 0:2 * P],
                                      flat(actT[i][0][:, :, :]).bitcast(F32), ALU.subtract).then_inc(actT_lo, 1)
                if exists(j + 1):
                    i = (r + 1) % 2
                    dve.wait_ge(xgT_hi, j + 2)
                    wait(dve, gu_done, j)
                    dve.tensor_tensor(flat(xgT[i][1][:, :, :, :]), flat(p_xt[:, i, :, :, :]),
                                      flat(xgT[i][0][:, :, :, :]).bitcast(F32), ALU.subtract).then_inc(xgT_lo, 1)
            stage_b(dve, group, before=1, after=2)

            def total(b, r, loads):
                dve.wait_ge(y_back[r], loads)
                for k in range(TOP_K):
                    for t in range(ST):
                        if k:
                            dve.wait_ge(z_step, ST * TOP_K * b + ST * k + t - 1)
                        dve.scalar_tensor_tensor(z[r][:, t, :], y_in[r][:, t, k, :],
                                                 share[:, bass.ds(ST * b + t, 1), k], z[r][:, t, :],
                                                 ALU.mult, ALU.add).then_inc(z_step, 1)

            for r in range(4):
                total(r, r, 32)
            if B > 4:
                with dve.Fori(1, B // 4) as q:
                    for r in range(4):
                        total(4 * q + r, r, 32 * (q + 1))

        @block.tensor
        def _(pe):
            pe.wait_ge(consts_set, 15)
            pe.wait_ge(const_in, 16 * N_CONST)
            for k in range(KT):
                last = pe.transpose(p_x[:, k * E:(k + 1) * E], gate_rows[:, k * P:(k + 1) * P], ident[0:E, 0:E])
            last.then_inc(gate_t, 1)

            PASSES = ((0, 0), (0, 1), (1, 0))

            def transpose_rows(dst, src):
                for k in range(KT):
                    for t in range(ST):
                        mm = pe.transpose(dst[:, k * S + t * P:k * S + (t + 1) * P],
                                          src(t)[:, k * P:(k + 1) * P], ident[:, :])
                return mm

            def project_cols(n, w, pair0):
                for j in range(2):
                    c = (pair0 + j) * P
                    i = 0
                    for k in range(KT):
                        for a, r in PASSES:
                            mm = pe.matmul(proj_bank(n)[:, j * S:(j + 1) * S], wp[a][:, w, k, c:c + P],
                                           rowsT[w // 3][r][:, k, :], start=(i == 0), stop=(i == 5))
                            i += 1
                mm.then_inc(proj_done, 1)

            def project_rows(n, w, t):
                i = 0
                for k in range(KT):
                    for r, a in PASSES:
                        mm = pe.matmul(proj_bank(n), rowsT[w // 3][r][:, k, t * P:(t + 1) * P], wp[a][:, w, k, :],
                                       start=(i == 0), stop=(i == 5))
                        i += 1
                mm.then_inc(proj_done, 1)

            def project(b, n):
                if n < 4:
                    wait(pe, exp_done, 4 * (STEPS * b - 1 + n // 2))
                elif n < 8:
                    pe.wait_ge(proj_out, PROJS * b + n - 3)
                    pe.wait_ge(proj_lo, 8 * b + n - 3)
                elif n < 10:
                    pe.wait_ge(proj_lo, 8 * b + n - 3)
                elif n == 10:
                    wait(pe, mid_set, b)
                else:
                    pe.wait_ge(rowsT_lo, 2 * b + 2)
                w = n // 2
                if isinstance(b, int) and b == 0:
                    pe.wait_ge(early_lo, w + 1)
                if w in (2, 5):
                    project_rows(n, w, n % 2)
                else:
                    project_cols(n, w, 2 * (n % 2))

            def scores(b, u):
                p, d = u // 2, u % 2
                if u < 2:
                    pe.wait_ge(proj_lo, 8 * b + 6 + 2 * u)
                else:
                    pe.wait_ge(exp_done, 4 * (STEPS * b + u - 1))
                for t in range(ST):
                    for i, (q, k) in enumerate(PASSES):
                        for h in range(2):
                            r = HEAD_DIM * h
                            mm = pe.matmul(p_s[:, 2 * d + h, t * S:(t + 1) * S],
                                           qT[d][q][r:r + HEAD_DIM, p, t * P:(t + 1) * P],
                                           kT[d][k][r:r + HEAD_DIM, p, :], start=(i == 0), stop=(i == 2))
                mm.then_inc(scores_done, 1)

            def probs_t(b, u):
                pe.wait_ge(normed_p, 3 * (STEPS * b + u + 1))
                pe.wait_ge(normed_v, STEPS * b + u + 1)
                if u == 0:
                    pe.wait_ge(proj_out, PROJS * (b + 1))
                    wait(pe, moeT_lo, b)
                else:
                    pe.wait_ge(pt_out_a, STEPS * b + u)
                    pe.wait_ge(pt_out_b, STEPS * b + u)
                for h in range(2):
                    for k in range(ST):
                        for t in range(ST):
                            mm = pe.transpose(p_pt[:, h, k * S + t * P:k * S + (t + 1) * P],
                                              probs[u % 2][:, h, t, k * P:(k + 1) * P], ident[:, :])
                    mm.then_inc(pt_done, 1)

            def attend(b, u):
                p, d = u // 2, u % 2
                pe.wait_ge(pt_out_a, STEPS * b + u + 1)
                pe.wait_ge(pt_out_b, STEPS * b + u + 1)
                if d == 0 and p:
                    pe.wait_ge(attn_out, PAIRS * b + p)
                for k in range(ST):
                    for h in range(2):
                        r = HEAD_DIM * h
                        c = p * P + r
                        mm = pe.matmul(p_av[r:r + HEAD_DIM, 0:S], val[d][:, k, c:c + HEAD_DIM], probsT[:, h, k, :],
                                       start=(d == 0 and k == 0), stop=(d == 1 and k == ST - 1),
                                       skip_group_check=True)
                mm.then_inc(av_done, 1)

            def context_t(b):
                pe.wait_ge(ctx_landed, 16 * (b + 1))
                transpose_rows(p_x, lambda t: rows[:, t, :]).then_inc(ctx_t, 1)

            def out_project(b):
                pe.wait_ge(attn_out, PAIRS * (b + 1))
                if isinstance(b, int) and b == 0:
                    pe.wait_ge(wout_in, 16)
                for t in range(ST):
                    for c in range(PAIRS):
                        mm = pe.matmul(p_av[:, t * D:(t + 1) * D], attnT[:, c, t * P:(t + 1) * P], wout[:, c, :],
                                       start=(c == 0), stop=(c == PAIRS - 1))
                mm.then_inc(outp_done, 1)

            def logits(m):
                pe.wait_ge(moeT_lo, m + 1)
                for t in range(ST):
                    n = 0
                    for k in range(KT):
                        for r, a in PASSES:
                            mm = pe.matmul(p_x[:, t * E:(t + 1) * E], moeT[r][:, k, t * P:(t + 1) * P],
                                           wgate[a][:, k, :], start=(n == 0), stop=(n == 5))
                            n += 1
                mm.then_inc(logits_done, 1)

            def places(m):
                pe.wait_ge(router_step, ROUTER_STEPS * m + 12)
                pe.matmul(p_x[:, 64:64 + E], before[:, :], chosen_b[:, 0, :], start=True, stop=True)
                pe.matmul(p_x[:, 64 + E:64 + 2 * E], before[:, :], chosen_b[:, 1, :], start=True, stop=False)
                pe.matmul(p_x[:, 64 + E:64 + 2 * E], ones[:, :], chosen_b[:, 0, :], start=False, stop=True)
                pe.matmul(p_x[:, 96:96 + E], ones[:, :], chosen_b[:, 0, :], start=True, stop=False)
                pe.matmul(p_x[:, 96:96 + E], ones[:, :], chosen_b[:, 1, :], start=False,
                          stop=True).then_inc(places_done, 1)

            def iteration(b, cur, prev, following):
                pb = b - 1
                if cur:
                    if isinstance(b, int) and b == 0:
                        pe.wait_ge(gate_lo, 1)
                        context_t(0)
                    pe.wait_ge(rowsT_lo, 2 * b + 1)
                    project(b, 0)
                if prev:
                    attend(pb, STEPS - 3)
                    probs_t(pb, STEPS - 2)
                if cur:
                    project(b, 1)
                if prev:
                    attend(pb, STEPS - 2)
                if cur:
                    project(b, 2)
                if prev:
                    probs_t(pb, STEPS - 1)
                if cur:
                    project(b, 3)
                if prev:
                    attend(pb, STEPS - 1)
                if cur:
                    pe.wait_ge(ln1_set, b + 1)
                    wait(pe, pt_out_a, STEPS * b)
                    transpose_rows(p_pt[:, 0, :], lambda t: rows[:, t, :]).then_inc(x_t, 1)
                if prev:
                    out_project(pb)
                if cur:
                    project(b, 4)
                    project(b, 5)
                    pe.wait_ge(rowsT_lo, 2 * b + 2)
                    project(b, 6)
                if prev:
                    pe.wait_ge(ln2_set, pb + 1)
                    pe.wait_ge(pt_out_b, STEPS * b)
                    transpose_rows(p_pt[:, 1, :], lambda t: routed[:, t, 0, 0:D]).then_inc(moe_t, 1)
                if cur:
                    project(b, 7)
                if prev:
                    logits(pb)
                if cur:
                    scores(b, 0)
                    for n in range(8, 11):
                        project(b, n)
                    scores(b, 1)
                    project(b, 11)
                    for u in range(2, STEPS):
                        scores(b, u)
                        if prev and u == 3:
                            places(pb)
                        if u >= 3:
                            attend(b, u - 3)
                        probs_t(b, u - 2)
                        if following and u == 5:
                            wait(pe, router_step, ROUTER_STEPS * b)
                            context_t(b + 1)
                else:
                    places(pb)

            stage_a(pe, iteration)

            pe.wait_ge(table_in, 16)
            pe.wait_ge(middle_hi, MIDDLE)
            pe.wait_ge(late_lo, LATE)

            def expert_of(j):
                return pe.value_load(table_row[0:1, 1, bass.ds(j, 1)], min_val=0, max_val=E - 1)

            experts = {}

            def group(j, r):
                if exists(j - 2) and r < 2:
                    experts[(r - 2) % LOADS] = expert_of(j - 2)
                if exists(j + 1):
                    i = (r + 1) % 2
                    pe.wait_ge(xg_in[(r + 1) % LOADS], xg_loads(j + 1, r + 1))
                    wait(pe, xgT_lo, j)
                    for n in range(2):
                        for k in range(KT):
                            mm = pe.transpose(p_xt[:, i, n, k, :], xg[(r + 1) % LOADS][:, n, k * P:(k + 1) * P], ident[:, :])
                    mm.then_inc(xg_t, 1)
                if exists(j):
                    i = r % 2
                    experts[r] = expert_of(j)
                    pe.wait_ge(xgT_lo, j + 1)
                    wait(pe, act_set, j - 1)
                    for n in range(2):
                        m = 0
                        for k in range(KT):
                            for h, a in PASSES:
                                mm = pe.matmul(p_gu[:, i, n, :], xgT[i][h][:, n, k, :],
                                               wgu[a][:, bass.ds(experts[r], 1), k, :, :].rearrange("p e g i -> p (e g i)"),
                                               start=(m == 0), stop=(m == 5))
                                m += 1
                    mm.then_inc(gu_done, 1)
                if exists(j - 1):
                    i = (r + 1) % 2
                    pe.wait_ge(act_set, j)
                    wait(pe, actT_lo, j - 2)
                    for n in range(2):
                        mm = pe.transpose(p_at[:, i, n * P:(n + 1) * P], gated[i][:, n, :], ident[:, :])
                    mm.then_inc(act_t, 1)
                if exists(j - 2):
                    i = r % 2
                    pe.wait_ge(actT_lo, j - 1)
                    wait(pe, y_set, j - 3)
                    for n in range(2):
                        for m, (h, a) in enumerate(PASSES):
                            mm = pe.matmul(p_y[:, i, n, :], actT[i][h][:, n, :],
                                           wdn[a][:, bass.ds(experts[(r - 2) % LOADS], 1), :].rearrange("p e d -> p (e d)"),
                                           start=(m == 0), stop=(m == 2))
                    mm.then_inc(down_done, 1)

            def xg_loads(j, r):
                return 16 // LOADS * (j - r % LOADS) + 16

            stage_b(pe, group, before=1, after=2)


_INS = ['x', 'ctx_1024', 'L0_xattn_Wq1', 'L0_xattn_Wk1', 'L0_xattn_Wv1', 'L0_xattn_Wq2', 'L0_xattn_Wk2',
        'L0_xattn_Wv2', 'L0_xattn_alpha_attn', 'L0_xattn_Wout', 'L0_xattn_bout', 'L0_ffn_gate_w', 'L0_ffn_w1',
        'L0_ffn_w3', 'L0_ffn_w2']


def kernel(**inputs):
    import numpy as _np
    import concourse.bacc as _bacc
    from concourse import mybir as _mybir
    from concourse.bass_utils import run_bass_kernel_spmd as _run

    nc = _bacc.Bacc("TRN2", target_bir_lowering=False, num_devices=1)
    arrays, args = {}, []
    for name in _INS:
        a = _np.ascontiguousarray(inputs[name])
        arrays[f"in_{name}_dram"] = a
        args.append(nc.dram_tensor(f"in_{name}_dram", a.shape, _mybir.dt.from_np(a.dtype), kind="ExternalInput").ap())
    shape = _np.shape(inputs["x"])
    args.append(nc.dram_tensor("out_0_dram", shape, _mybir.dt.float32, kind="ExternalOutput").ap())
    xattn_moe_kernel(nc, *args)
    r = _run(nc, [arrays], core_ids=[0])
    return r.results[0]["out_0_dram"]
```
